# Optimizing a Trainium2 kernel written in Bass

```python
import numpy as np
import jax
import jax.numpy as jnp

def _softmax(x, axis=-1):
    return jax.nn.softmax(x, axis=axis)

def _gelu(x):
    return jax.nn.gelu(x, approximate=True)

def _silu(x):
    return jax.nn.silu(x)

def _sigmoid(x):
    return jax.nn.sigmoid(x)

def _layernorm(x, axis=-1, eps=1e-05):
    m = jnp.mean(x, axis=axis, keepdims=True)
    v = jnp.var(x, axis=axis, keepdims=True)
    return (x - m) / jnp.sqrt(v + eps)

def _scatter_add(tgt, idx, src, axis=0):
    return tgt.at[idx].add(src)

def _segment_sum(src, seg, n):
    return jax.ops.segment_sum(src, seg, n)
kernel_name = 'mk_sandwich_d1_jaxref_r8_f753cc'

def setup_inputs(seed: int=0):
    np.random.seed(seed)
    _w = jnp.asarray

    def _L0_attn_setup():
        import jax, jax.numpy as jnp
        import numpy as np
        B, T, IN_DIM, EMB = (8, 256, 128, 128)
        NEG_INF = -1e+30
        key = jax.random.key(seed)
        ks = jax.random.split(key, 7)
        s = 1.0 / np.sqrt(IN_DIM)
        return {'x': jax.random.normal(ks[0], (B, T, IN_DIM), dtype=jnp.float32), 'Wq': jax.random.normal(ks[1], (IN_DIM, EMB), dtype=jnp.float32) * s, 'bq': jax.random.normal(ks[2], (EMB,), dtype=jnp.float32) * 0.01, 'Wk': jax.random.normal(ks[3], (IN_DIM, EMB), dtype=jnp.float32) * s, 'bk': jax.random.normal(ks[4], (EMB,), dtype=jnp.float32) * 0.01, 'Wv': jax.random.normal(ks[5], (IN_DIM, EMB), dtype=jnp.float32) * s, 'bv': jax.random.normal(ks[6], (EMB,), dtype=jnp.float32) * 0.01}
    _L0_attn_in = _L0_attn_setup()

    def _L0_ffn_setup():
        import jax, jax.numpy as jnp
        import numpy as np
        HIDDEN = 128
        N_EXPERTS = 8
        TOP_K = 2
        INTER = 176
        N_SHARED = 2
        SCALE = 1.0
        key = jax.random.key(seed)
        ks = jax.random.split(key, 9)
        s_h = 1.0 / np.sqrt(HIDDEN)
        s_i = 1.0 / np.sqrt(INTER)
        x = jax.random.normal(ks[0], (2, 256, HIDDEN), dtype=jnp.float32)
        gate_w = jax.random.uniform(ks[1], (N_EXPERTS, HIDDEN), jnp.float32, -s_h, s_h)
        wg = jax.random.uniform(ks[2], (N_EXPERTS, HIDDEN, INTER), jnp.float32, -s_h, s_h)
        wu = jax.random.uniform(ks[3], (N_EXPERTS, HIDDEN, INTER), jnp.float32, -s_h, s_h)
        wd = jax.random.uniform(ks[4], (N_EXPERTS, INTER, HIDDEN), jnp.float32, -s_i, s_i)
        si = INTER * N_SHARED
        s_si = 1.0 / np.sqrt(si)
        swg = jax.random.uniform(ks[5], (HIDDEN, si), jnp.float32, -s_h, s_h)
        swu = jax.random.uniform(ks[6], (HIDDEN, si), jnp.float32, -s_h, s_h)
        swd = jax.random.uniform(ks[7], (si, HIDDEN), jnp.float32, -s_si, s_si)
        return {'x': x, 'gate_w': gate_w, 'wg': wg, 'wu': wu, 'wd': wd, 'swg': swg, 'swu': swu, 'swd': swd}
    _L0_ffn_in = _L0_ffn_setup()
    _d = {'L0_attn_x': _L0_attn_in['x'], 'L0_attn_Wq': _L0_attn_in['Wq'], 'L0_attn_bq': _L0_attn_in['bq'], 'L0_attn_Wk': _L0_attn_in['Wk'], 'L0_attn_bk': _L0_attn_in['bk'], 'L0_attn_Wv': _L0_attn_in['Wv'], 'L0_attn_bv': _L0_attn_in['bv'], 'L0_ffn_gate_w': _L0_ffn_in['gate_w'], 'L0_ffn_wg': _L0_ffn_in['wg'], 'L0_ffn_wu': _L0_ffn_in['wu'], 'L0_ffn_wd': _L0_ffn_in['wd'], 'L0_ffn_swg': _L0_ffn_in['swg'], 'L0_ffn_swu': _L0_ffn_in['swu'], 'L0_ffn_swd': _L0_ffn_in['swd']}
    _x0 = _d['L0_attn_x']
    _d['L0_attn_x'] = jax.random.normal(jax.random.fold_in(jax.random.key(seed), 1), (4, 1024, 128), dtype=_x0.dtype)
    del _x0
    return _d

def reference(L0_attn_x, L0_attn_Wq, L0_attn_bq, L0_attn_Wk, L0_attn_bk, L0_attn_Wv, L0_attn_bv, L0_ffn_gate_w, L0_ffn_wg, L0_ffn_wu, L0_ffn_wd, L0_ffn_swg, L0_ffn_swu, L0_ffn_swd):

    def _L0_attn_ref(x, Wq, bq, Wk, bk, Wv, bv):
        import jax, jax.numpy as jnp
        import numpy as np
        B, T, IN_DIM, EMB = (8, 256, 128, 128)
        NEG_INF = -1e+30
        q = x @ Wq + bq
        k = x @ Wk + bk
        v = x @ Wv + bv
        scale = jnp.asarray(EMB, x.dtype) ** 0.5
        scores = jnp.einsum('btd,bsd->bts', q, k) / scale
        Tq = scores.shape[-2]
        causal = jnp.tril(jnp.ones((Tq, Tq), dtype=bool))
        scores = jnp.where(causal, scores, jnp.asarray(NEG_INF, scores.dtype))
        m = jnp.max(scores, axis=(-2, -1), keepdims=True)
        e = jnp.exp(scores - m)
        w = e / jnp.sum(e, axis=(-2, -1), keepdims=True)
        return jnp.einsum('bts,bsd->btd', w, v)

    def _L0_ffn_ref(x, gate_w, wg, wu, wd, swg, swu, swd):
        import jax, jax.numpy as jnp
        import numpy as np
        HIDDEN = 128
        N_EXPERTS = 8
        TOP_K = 2
        INTER = 176
        N_SHARED = 2
        SCALE = 1.0
        B, S, H = x.shape
        xf = x.reshape(-1, H)
        T = xf.shape[0]
        logits = xf.astype(jnp.float32) @ gate_w.astype(jnp.float32).T
        scores = jax.nn.softmax(logits, axis=-1)
        topw, topi = jax.lax.top_k(scores, TOP_K)
        denom = topw.sum(axis=-1, keepdims=True) + 1e-20
        topw = topw / denom * SCALE
        wdense = jnp.zeros((T, N_EXPERTS), jnp.float32).at[jnp.arange(T)[:, None], topi].set(topw)
        hg = jnp.einsum('th,ehi->eti', xf, wg)
        hu = jnp.einsum('th,ehi->eti', xf, wu)
        eo = jnp.einsum('eti,eih->eth', jax.nn.silu(hg) * hu, wd)
        y = jnp.einsum('te,eth->th', wdense, eo)
        shared = jax.nn.silu(xf @ swg) * (xf @ swu) @ swd
        return (y + shared).reshape(B, S, H)
    x = L0_attn_x
    x = x + _layernorm(_L0_attn_ref(_layernorm(x, axis=-1), L0_attn_Wq, L0_attn_bq, L0_attn_Wk, L0_attn_bk, L0_attn_Wv, L0_attn_bv), axis=-1)
    x = x + _layernorm(_L0_ffn_ref(_layernorm(x, axis=-1), L0_ffn_gate_w, L0_ffn_wg, L0_ffn_wu, L0_ffn_wd, L0_ffn_swg, L0_ffn_swu, L0_ffn_swd), axis=-1)
    return x

_drawn_inputs = setup_inputs


def setup_inputs(seed=0):
    import zlib

    import numpy as np

    out = dict(_drawn_inputs(seed))
    spreads = {}
    factors = {'L0_attn_bq': 23.945, 'L0_attn_bk': 32.13, 'L0_attn_bv': 2.696}
    for name, (base, spread) in spreads.items():
        noise = np.random.default_rng([zlib.crc32(name.encode()), seed]).standard_normal(out[name].shape)
        drawn = base * np.exp(spread * noise) if base else spread * noise
        out[name] = jnp.asarray(drawn.astype(out[name].dtype))
    for name, factor in factors.items():
        out[name] = (out[name] * factor).astype(out[name].dtype)
    return out
```

```python
from contextlib import ExitStack

import numpy as np

import concourse.bass as bass
from concourse import mybir

P = 128
NB, T, D = 4, 1024, 128
NT = T // P
HALF = 512
NH = T // HALF
TPH = HALF // P
NE, I, NS = 8, 176, 2
ROUTED, SHARED = NE * I, NS * I
FF = ROUTED + SHARED
NR = ROUTED // P
NC = -(-FF // P)
LASTC = FF - (NC - 1) * P
STEPS = NH * NC
ROUTED_STEPS = NH * NR
EPS = 1e-5
SCALE = float(D) ** -0.5
NEG = -1e30

UNITS = [(h, j) for h in range(NH) for j in range(TPH * (h + 1))]
NU = len(UNITS)
UNIT_COL = [max(0, P * j - HALF * h) for h, j in UNITS]
UNIT_AT = [sum(HALF - c for c in UNIT_COL[:u]) for u in range(NU)]
E_COLS = sum(HALF - c for c in UNIT_COL)

F32 = mybir.dt.float32
F32R = mybir.dt.float32r
BF16 = mybir.dt.bfloat16
ALU = mybir.AluOpType
ACT = mybir.ActivationFunctionType
AX = mybir.AxisListType


def rows(c):
    return LASTC if c == NC - 1 else P


def wb_count(k):
    return (k // NC) * NR + min(k % NC + 1, NR)


def sandwich(nc, x, Wq, bq, Wk, bk, Wv, bv, gate_w, wg, wu, wd, swg, swu, swd, out):
    ctx = ExitStack()
    with ctx:
        def sb(name, shape, dt=F32):
            return ctx.enter_context(nc.sbuf_tensor(name, shape, dt))

        def sem(name):
            return ctx.enter_context(nc.semaphore(name))

        ident = sb("ident", [P, P])
        identb = sb("identb", [P, P], BF16)
        ones = sb("ones", [P, P])
        maskb = sb("maskb", [P, P], BF16)
        before = sb("before", [P, NE, NE])
        neg_half = sb("neg_half", [P, NT])
        sel_two = sb("sel_two", [2 * NE, 2, ROUTED], BF16)
        sel = sb("sel", [2 * NE, ROUTED], F32R)
        Wqk_s = sb("Wqk_s", [P, 2, P])
        WqkT = sb("WqkT", [P, 2, P])
        Wv_s = sb("Wv_s", [P, P])
        bqk = sb("bqk", [P, 2])
        bk_rep = sb("bk_rep", [P, P])
        bv_b = sb("bv_b", [P, P])
        gw_s = sb("gw_s", [NE, P])
        A_h, A_l = sb("A_h", [P, P], F32R), sb("A_l", [P, P], F32R)
        Wv_h, Wv_l = sb("Wv_h", [P, P], F32R), sb("Wv_l", [P, P], F32R)
        wkbq_s = sb("wkbq_s", [P, 2])
        wkbq_h, wkbq_l = sb("wkbq_h", [P, 2], F32R), sb("wkbq_l", [P, 2], F32R)
        wqbk = sb("wqbk", [P, 1])
        bqbk = sb("bqbk", [P, 1])
        gwT_s = sb("gwT_s", [P, NE])
        gwT_h, gwT_l = sb("gwT_h", [P, NE], F32R), sb("gwT_l", [P, NE], F32R)
        Wg_s, Wu_s, Wd_s = sb("Wg_s", [P, FF]), sb("Wu_s", [P, FF]), sb("Wd_s", [P, NC, P])
        Wg_h, Wg_l = sb("Wg_h", [P, FF], F32R), sb("Wg_l", [P, FF], F32R)
        Wu_h, Wu_l = sb("Wu_h", [P, FF], F32R), sb("Wu_l", [P, FF], F32R)
        Wd_h, Wd_l = sb("Wd_h", [P, NC, P], F32R), sb("Wd_l", [P, NC, P], F32R)

        X = sb("X", [P, NB, NT, P])
        Y = sb("Y", [P, NT, P])
        YT_h, YT_l = sb("YT_h", [P, T], F32R), sb("YT_l", [P, T], F32R)
        KK_h, KK_l = sb("KK_h", [P, T], F32R), sb("KK_l", [P, T], F32R)
        V = sb("V", [P, NT, P])
        VP = sb("VP", [P, NU, P])
        E = sb("E", [P, E_COLS])
        OT = sb("OT", [P, T])
        Y2_h, Y2_l = sb("Y2_h", [P, T], F32R), sb("Y2_l", [P, T], F32R)
        st = sb("st", [P, NT, 6])
        mu, dif, vs = sb("mu", [P, NT]), sb("dif", [P, NT]), sb("vs", [P, NT])
        ve = sb("ve", [P, NT])
        rs = sb("rs", [P, NT])
        nmr = sb("nmr", [P, NT])
        nmax = sb("nmax", [P, NU])
        nbias = sb("nbias", [P, NU])
        rsum = sb("rsum", [P, NU])
        cs = sb("cs", [P, NT])
        val = sb("val", [P, NU])
        mx = sb("mx", [P, 1])
        m1 = sb("m1", [1, 1])
        nmg = sb("nmg", [P, 1])
        fac = sb("fac", [P, NU])
        rf = sb("rf", [P, NU])
        zp = sb("zp", [P, 1])
        zs = sb("zs", [P, 1])
        ez = sb("ez", [P, 1])
        scratch = sb("scratch", [P, 1])
        gmax = sb("gmax", [P, NT])
        lg = sb("lg", [P, NT, NE])
        eg = sb("eg", [P, NT, NE])
        gsum = sb("gsum", [P, NT])
        grec = sb("grec", [P, NT])
        pg = sb("pg", [P, NT, NE])
        cmp_gt = sb("cmp_gt", [P, NT, NE, NE])
        cmp_eq = sb("cmp_eq", [P, NT, NE, NE])
        rank = sb("rank", [P, NT, NE])
        wsel = sb("wsel", [P, NT, NE])
        wn = sb("wn", [P, NT, NE])
        whl = sb("whl", [P, NT, 2, NE], F32R)
        wT = sb("wT", [2 * NE, T], F32R)
        S = sb("S", [P, 2, HALF])
        TU = sb("TU", [P, 2, HALF])
        H = sb("H", [P, 2, HALF])
        H_h, H_l = sb("H_h", [P, 3, HALF], F32R), sb("H_l", [P, 3, HALF], F32R)
        OF = sb("OF", [P, HALF])
        fst = sb("fst", [P, TPH, 6])
        fmu, fdif, fvs = sb("fmu", [P, TPH]), sb("fdif", [P, TPH]), sb("fvs", [P, TPH])
        fve = sb("fve", [P, TPH])
        frs = sb("frs", [P, TPH])
        fnmr = sb("fnmr", [P, TPH])
        FX = sb("FX", [P, 2, TPH, P])

        def bank(name):
            return ctx.enter_context(nc.psum_tensor(name, [P, HALF], F32))

        SC = [bank("SC0"), bank("SC1")]
        TP = bank("TP")
        GB, UB, WB, DB, XB = bank("GB"), bank("UB"), bank("WB"), bank("DB"), bank("XB")

        x_loaded = sem("x_loaded")
        small_loaded = sem("small_loaded")
        wg_loaded = sem("wg_loaded")
        wu_loaded = sem("wu_loaded")
        wd_loaded = sem("wd_loaded")
        out_stored = sem("out_stored")
        consts = sem("consts")
        pool_step = sem("pool_step")
        prep_ps = sem("prep_ps")
        prep_act = sem("prep_act")
        prep_dve = sem("prep_dve")
        wgu_split = sem("wgu_split")
        wd_split = sem("wd_split")
        var1 = sem("var1")
        pow1 = sem("pow1")
        y_ready = sem("y_ready")
        yT_ps = sem("yT_ps")
        yhi = sem("yhi")
        ylo = sem("ylo")
        kk_ps = sem("kk_ps")
        khi = sem("khi")
        klo = sem("klo")
        v_ps = sem("v_ps")
        v_ev = sem("v_ev")
        c_ps = sem("c_ps")
        c_ev = sem("c_ev")
        sc_ps = sem("sc_ps")
        nb = sem("nb")
        exps_done = sem("exps_done")
        mx_ready = sem("mx_ready")
        maxT_ps = sem("maxT_ps")
        m1_ready = sem("m1_ready")
        maxB_ps = sem("maxB_ps")
        nmg_ready = sem("nmg_ready")
        fexp = sem("fexp")
        zp_ready = sem("zp_ready")
        z_ps = sem("z_ps")
        vp_ready = sem("vp_ready")
        ez_ready = sem("ez_ready")
        pv_ps = sem("pv_ps")
        o_ev = sem("o_ev")
        oT_ps = sem("oT_ps")
        var2 = sem("var2")
        pow2 = sem("pow2")
        nmr2 = sem("nmr2")
        ox_ready = sem("ox_ready")
        x1_ready = sem("x1_ready")
        var3 = sem("var3")
        pow3 = sem("pow3")
        y2_ready = sem("y2_ready")
        y2T_ps = sem("y2T_ps")
        y2hi = sem("y2hi")
        y2lo = sem("y2lo")
        gate_ps = sem("gate_ps")
        lg_ready = sem("lg_ready")
        gexp = sem("gexp")
        whl_ready = sem("whl_ready")
        wT_ps = sem("wT_ps")
        wT_ready = sem("wT_ready")
        g_ps = sem("g_ps")
        u_ps = sem("u_ps")
        wb_ps = sem("wb_ps")
        d_ps = sem("d_ps")
        s_ready = sem("s_ready")
        u_used = sem("u_used")
        h_ready = sem("h_ready")
        hi_ready = sem("hi_ready")
        lo_ready = sem("lo_ready")
        fo_ev = sem("fo_ev")
        f_step = sem("f_step")
        fT_ps = sem("fT_ps")
        var4 = sem("var4")
        pow4 = sem("pow4")
        nmr4 = sem("nmr4")
        fx_ready = sem("fx_ready")
        out_ready = sem("out_ready")
        dve_step = sem("dve_step")

        def split3(pe, out_ap, wh, wl, xh, xl):
            nc.tensor.matmul(out_ap, wh, xh, start=True, stop=False)
            nc.tensor.matmul(out_ap, wh, xl, start=False, stop=False)
            return nc.tensor.matmul(out_ap, wl, xh, start=False, stop=True)

        block = ctx.enter_context(nc.Block())

        @block.sync
        def _(sp):
            xt = x.rearrange("b (t p) d -> b p t d", p=P)
            ot = out.rearrange("b (g t p) d -> b g p t d", g=NH, p=P)
            sp.dma_start(X[:, 0, :, :], xt[0]).then_inc(x_loaded, 16)
            sp.dma_start(Wqk_s[:, 0, :], Wq).then_inc(small_loaded, 16)
            sp.dma_start(Wqk_s[:, 1, :], Wk).then_inc(small_loaded, 16)
            sp.dma_start(bqk[:, 0:1], bq.rearrange("(p o) -> p o", o=1)).then_inc(small_loaded, 16)
            sp.dma_start(bqk[:, 1:2], bk.rearrange("(p o) -> p o", o=1)).then_inc(small_loaded, 16)
            sp.dma_start(gw_s[:, :], gate_w).then_inc(small_loaded, 16)
            sp.dma_start(Wv_s[:, :], Wv).then_inc(small_loaded, 16)
            sp.dma_start(bv_b[:, :], bv.rearrange("(o d) -> o d", o=1).to_broadcast([P, P])
                         ).then_inc(small_loaded, 16)
            rt = slice(0, ROUTED)
            sh = slice(ROUTED, FF)
            sp.dma_start(Wg_s[:, rt].rearrange("p (e i) -> p e i", e=NE),
                         wg.rearrange("e h i -> h e i")).then_inc(wg_loaded, 16)
            sp.dma_start(Wg_s[:, sh], swg).then_inc(wg_loaded, 16)
            sp.dma_start(Wu_s[:, rt].rearrange("p (e i) -> p e i", e=NE),
                         wu.rearrange("e h i -> h e i")).then_inc(wu_loaded, 16)
            sp.dma_start(Wu_s[:, sh], swu).then_inc(wu_loaded, 16)
            sp.dma_start(Wd_s[:, 0:NR, :], wd.rearrange("e i h -> (e i) h").rearrange("(c p) h -> p c h", p=P)
                         ).then_inc(wd_loaded, 16)
            full = NC - 1 - NR
            sp.dma_start(Wd_s[:, NR:NC - 1, :], swd[0:full * P, :].rearrange("(c p) h -> p c h", p=P)
                         ).then_inc(wd_loaded, 16)
            sp.dma_start(Wd_s[0:LASTC, NC - 1, :], swd[full * P:SHARED, :]).then_inc(wd_loaded, 16)
            for b in range(1, NB):
                sp.wait_ge(x_loaded, 16 * b)
                sp.dma_start(X[:, b, :, :], xt[b]).then_inc(x_loaded, 16)
            for b in range(NB):
                for g in range(NH):
                    sp.wait_ge(out_ready, NH * b + g + 1)
                    sp.dma_start(ot[b, g], X[:, b, g * TPH:(g + 1) * TPH, :]).then_inc(out_stored, 16)
            sp.wait_ge(out_stored, 16 * NB * NH)

        @block.gpsimd
        def _(pool):
            n = [0]

            def step(ins):
                n[0] += 1
                ins.then_inc(pool_step, 1)
                pool.wait_ge(pool_step, n[0])

            step(nc.gpsimd.memset(ident[:, :], 0.0))
            step(nc.gpsimd.affine_select(out=ident[:, :], in_=ident[:, :], compare_op=ALU.not_equal, fill=1.0,
                                         base=0, pattern=[[-1, P]], channel_multiplier=1))
            nc.gpsimd.memset(neg_half[:, :], -0.5)
            nc.gpsimd.memset(ones[:, :], 1.0)
            step(nc.gpsimd.memset(maskb[:, :], 0.0))
            step(nc.gpsimd.affine_select(out=maskb[:, :], in_=maskb[:, :], compare_op=ALU.is_ge, fill=NEG,
                                         base=0, pattern=[[1, P]], channel_multiplier=-1))
            nc.gpsimd.tensor_copy(identb[:, :], ident[:, :]).then_inc(consts, 1)

            def power(dst, src, width):
                return nc.gpsimd.tensor_tensor(dst, src, neg_half[:, 0:width], ALU.pow)

            def pow_ln1(b):
                pool.wait_ge(var1, b + 1)
                power(rs[:, :], ve[:, :], NT).then_inc(pow1, 1)

            def pow_attention(b):
                pool.wait_ge(var2, b + 1)
                power(rs[:, :], ve[:, :], NT).then_inc(pow2, 1)

            def pow_ln2(b):
                pool.wait_ge(var3, b + 1)
                power(rs[:, :], ve[:, :], NT).then_inc(pow3, 1)

            pow_ln1(0)
            step(nc.gpsimd.memset(before[:, :, :], 1.0))
            step(nc.gpsimd.affine_select(out=before[:, :, :], in_=before[:, :, :], compare_op=ALU.is_ge, fill=0.0,
                                         base=-1, pattern=[[1, NE], [-1, NE]], channel_multiplier=0))
            step(nc.gpsimd.memset(sel_two[:, :, :], 1.0))
            step(nc.gpsimd.affine_select(out=sel_two[:, :, :], in_=sel_two[:, :, :], compare_op=ALU.is_ge, fill=0.0,
                                         base=0, pattern=[[ROUTED, 2], [1, ROUTED]], channel_multiplier=-I))
            step(nc.gpsimd.affine_select(out=sel_two[:, :, :], in_=sel_two[:, :, :], compare_op=ALU.is_ge, fill=0.0,
                                         base=I - 1, pattern=[[-ROUTED, 2], [-1, ROUTED]], channel_multiplier=I))
            nc.gpsimd.tensor_tensor(sel[:, :], sel_two[:, 0, :], sel_two[:, 1, :], ALU.add
                                    ).then_inc(consts, 1)

            def split(hi, lo, src):
                step(nc.gpsimd.tensor_copy(hi, src))
                return nc.gpsimd.tensor_tensor(lo, src, hi.bitcast(F32), ALU.subtract)

            pool.wait_ge(wg_loaded, 32)
            split(Wg_h[:, :], Wg_l[:, :], Wg_s[:, :]).then_inc(wgu_split, 1)
            pool.wait_ge(wu_loaded, 32)
            split(Wu_h[:, :], Wu_l[:, :], Wu_s[:, :]).then_inc(wgu_split, 1)
            pow_attention(0)
            pow_ln2(0)
            pool.wait_ge(wd_loaded, 48)
            split(Wd_h[:, 0:NC - 1, :], Wd_l[:, 0:NC - 1, :], Wd_s[:, 0:NC - 1, :])
            split(Wd_h[0:LASTC, NC - 1, :], Wd_l[0:LASTC, NC - 1, :], Wd_s[0:LASTC, NC - 1, :]
                  ).then_inc(wd_split, 1)

            def ffn_step(b, k):
                r = rows(k % NC)
                pool.wait_ge(h_ready, b * STEPS + k + 1)
                pool.wait_ge(hi_ready, b * STEPS + k + 1)
                if k >= 3:
                    pool.wait_ge(d_ps, b * STEPS + k - 2)
                nc.gpsimd.tensor_tensor(H_l[0:r, k % 3, :], H[0:r, k % 2, :], H_h[0:r, k % 3, :].bitcast(F32),
                                        ALU.subtract).then_inc(lo_ready, 1)

            def ffn_pow(b, g):
                pool.wait_ge(var4, NH * b + g + 1)
                power(frs[:, :], fve[:, :], TPH).then_inc(pow4, 1)

            def ffn(b):
                for k in range(STEPS):
                    ffn_step(b, k)
                    if k == NC + 3:
                        ffn_pow(b, 0)
                ffn_pow(b, 1)

            with pool.Fori(1, NB) as b:
                ffn(b - 1)
                pow_ln1(b)
                pow_attention(b)
                pow_ln2(b)
            ffn(NB - 1)

        @block.tensor
        def _(pe):
            pe.wait_ge(consts, 1)
            pe.wait_ge(small_loaded, 16 * 7)
            nc.tensor.transpose(SC[0][:, 0:P], Wqk_s[:, 0, :], ident[:, :])
            nc.tensor.transpose(SC[0][:, P:2 * P], Wqk_s[:, 1, :], ident[:, :])
            nc.tensor.transpose(SC[0][:, 2 * P:2 * P + NE], gw_s[:, :], ident[0:NE, 0:NE]
                                ).then_inc(prep_ps, 1)
            pe.wait_ge(prep_act, 1)
            nc.tensor.matmul(SC[1][:, 0:P], WqkT[:, 1, :], WqkT[:, 0, :], start=True, stop=True)
            nc.tensor.matmul(SC[1][:, P:P + 1], WqkT[:, 0, :], bqk[:, 1:2], start=True, stop=True)
            nc.tensor.matmul(SC[1][:, P + 1:P + 2], WqkT[:, 1, :], bqk[:, 0:1], start=True, stop=True)
            nc.tensor.matmul(SC[1][:, P + 2:P + 3], bk_rep[:, :], bqk[:, 0:1], start=True, stop=True
                             ).then_inc(prep_ps, 1)

            def transposes(dst, src):
                for t in range(TPH):
                    last = nc.tensor.transpose(dst[:, t * P:(t + 1) * P], src(t), ident[:, :])
                return last

            def yT(b):
                for h in range(NH):
                    pe.wait_ge(y_ready, NH * b + h + 1)
                    transposes(SC[h], lambda t: Y[:, h * TPH + t, :]).then_inc(yT_ps, 1)

            def keys(b):
                for h in range(NH):
                    c = slice(h * HALF, (h + 1) * HALF)
                    pe.wait_ge(ylo, NH * b + h + 1)
                    split3(pe, [TP, SC[0]][h][:, :], A_h[:, :], A_l[:, :], YT_h[:, c], YT_l[:, c]
                           ).then_inc(kk_ps, 1)

            def values(b):
                for h in range(NH):
                    if h == 1:
                        pe.wait_ge(klo, NH * b + 1)
                    for t in range(TPH):
                        c = slice((h * TPH + t) * P, (h * TPH + t + 1) * P)
                        last = split3(pe, [SC[1], TP][h][:, t * P:(t + 1) * P],
                                      YT_h[:, c], YT_l[:, c], Wv_h[:, :], Wv_l[:, :])
                    last.then_inc(v_ps, 1)
                pe.wait_ge(klo, NH * b + 2)
                for t in range(NT):
                    c = slice(t * P, (t + 1) * P)
                    last = split3(pe, SC[0][:, 2 * t:2 * t + 2], YT_h[:, c], YT_l[:, c],
                                  wkbq_h[:, :], wkbq_l[:, :])
                last.then_inc(c_ps, 1)

            def scores(b, u):
                h, j = UNITS[u]
                c0 = UNIT_COL[u]
                if u == 0:
                    pe.wait_ge(c_ev, b + 1)
                elif u == 1:
                    pe.wait_ge(v_ev, NH * b + 1)
                else:
                    pe.wait_ge(exps_done, NU * b + u - 1)
                dst = SC[u % 2][:, c0:HALF]
                q = slice(h * HALF + c0, (h + 1) * HALF)
                kt = slice(j * P, (j + 1) * P)
                diag = j * P >= h * HALF
                nc.tensor.matmul(dst, KK_h[:, kt], YT_h[:, q], start=True, stop=False)
                nc.tensor.matmul(dst, KK_h[:, kt], YT_l[:, q], start=False, stop=False)
                last = nc.tensor.matmul(dst, KK_l[:, kt], YT_h[:, q], start=False, stop=not diag)
                if diag:
                    last = nc.tensor.matmul(SC[u % 2][:, c0:c0 + P], identb[:, :], maskb[:, :],
                                            start=False, stop=True)
                last.then_inc(sc_ps, 1)

            def maximum(b):
                pe.wait_ge(mx_ready, b + 1)
                nc.tensor.transpose(TP[0:1, 0:P], mx[:, :], ident[:, :]).then_inc(maxT_ps, 1)
                pe.wait_ge(m1_ready, b + 1)
                nc.tensor.matmul(TP[:, P:P + 1], ones[0:1, :], m1[:, :], start=True, stop=True
                                 ).then_inc(maxB_ps, 1)

            def attend(b):
                pe.wait_ge(exps_done, NU * (b + 1))
                pe.wait_ge(zp_ready, b + 1)
                nc.tensor.matmul(TP[:, P:P + 1], ones[:, :], zp[:, :], start=True, stop=True
                                 ).then_inc(z_ps, 1)
                for h in range(NH):
                    pe.wait_ge(vp_ready, NH * b + h + 1)
                    units = [u for u in range(NU) if UNITS[u][0] == h]
                    for u in units:
                        w = HALF - UNIT_COL[u]
                        last = nc.tensor.matmul(SC[h][:, UNIT_COL[u]:HALF], VP[:, u, :],
                                                E[:, UNIT_AT[u]:UNIT_AT[u] + w],
                                                start=u == units[0], stop=u == units[-1])
                    last.then_inc(pv_ps, 1)

            def oT(b):
                pe.wait_ge(ez_ready, b + 1)
                for h in range(NH):
                    pe.wait_ge(o_ev, NH * b + h + 1)
                    transposes([TP, SC[0]][h], lambda t: OT[:, (h * TPH + t) * P:(h * TPH + t + 1) * P]).then_inc(oT_ps, 1)

            def y2T(b):
                for h in range(NH):
                    pe.wait_ge(y2_ready, NH * b + h + 1)
                    transposes([SC[1], TP][h], lambda t: Y[:, h * TPH + t, :]).then_inc(y2T_ps, 1)

            def gate(b):
                pe.wait_ge(y2lo, NH * (b + 1))
                for t in range(NT):
                    c = slice(t * P, (t + 1) * P)
                    last = split3(pe, SC[0][:, NE * t:NE * (t + 1)], Y2_h[:, c], Y2_l[:, c],
                                  gwT_h[:, :], gwT_l[:, :])
                last.then_inc(gate_ps, 1)
                pe.wait_ge(whl_ready, b + 1)
                for h in range(NH):
                    for t in range(TPH):
                        last = nc.tensor.transpose([SC[1], TP][h][0:2 * NE, t * P:(t + 1) * P],
                                                   whl[:, h * TPH + t, :, :].rearrange("p a e -> p (a e)").bitcast(F32),
                                                   ident[:, :])
                    last.then_inc(wT_ps, 1)

            def down(b, k):
                c, r = k % NC, rows(k % NC)
                if c == 0 and k > 0:
                    pe.wait_ge(fo_ev, NH * b + 1)
                pe.wait_ge(lo_ready, b * STEPS + k + 1)
                for i, (w, hh) in enumerate([(Wd_h, H_h), (Wd_h, H_l), (Wd_l, H_h)]):
                    last = nc.tensor.matmul(DB[:, :], w[0:r, c, :], hh[0:r, k % 3, :],
                                            start=c == 0 and i == 0, stop=c == NC - 1 and i == 2)
                last.then_inc(d_ps, 1)

            def product_used(b, k):
                if k % NC < NR:
                    pe.wait_ge(u_used, b * ROUTED_STEPS + wb_count(k))
                else:
                    pe.wait_ge(h_ready, b * STEPS + k + 1)

            def ffn_step(b, k):
                g, c = divmod(k, NC)
                r = rows(c)
                ic = slice(c * P, c * P + r)
                tok = slice(g * HALF, (g + 1) * HALF)
                if k > 0:
                    pe.wait_ge(s_ready, b * STEPS + k)
                split3(pe, GB[0:r, :], Wg_h[:, ic], Wg_l[:, ic], Y2_h[:, tok], Y2_l[:, tok]
                       ).then_inc(g_ps, 1)
                if k > 0:
                    product_used(b, k - 1)
                split3(pe, UB[0:r, :], Wu_h[:, ic], Wu_l[:, ic], Y2_h[:, tok], Y2_l[:, tok]
                       ).then_inc(u_ps, 1)
                if c < NR:
                    if k > 0:
                        last_routed = k - 1 if c else k - 1 - (NC - NR)
                        pe.wait_ge(h_ready, b * STEPS + last_routed + 1)
                    nc.tensor.matmul(WB[:, :], sel[:, ic], wT[:, tok], start=True, stop=True
                                     ).then_inc(wb_ps, 1)
                if k >= 2:
                    down(b, k - 2)

            def fT(b, g):
                if g == 1:
                    pe.wait_ge(fx_ready, NH * b + g)
                pe.wait_ge(fo_ev, NH * b + g + 1)
                transposes(XB, lambda t: OF[:, t * P:(t + 1) * P]).then_inc(fT_ps, 1)

            def ffn(b):
                for k in range(STEPS):
                    ffn_step(b, k)
                    if k == NC + 2:
                        fT(b, 0)
                down(b, STEPS - 2)
                down(b, STEPS - 1)
                fT(b, 1)

            def attention(b):
                yT(b)
                keys(b)
                values(b)
                for u in range(NU):
                    scores(b, u)
                maximum(b)
                attend(b)
                oT(b)
                y2T(b)
                gate(b)

            pe.wait_ge(prep_dve, 1)
            attention(0)
            pe.wait_ge(wgu_split, 2)
            pe.wait_ge(consts, 2)
            pe.wait_ge(wd_split, 1)
            pe.wait_ge(wT_ready, 1)
            with pe.Fori(1, NB) as b:
                pe.wait_ge(wT_ready, b)
                ffn(b - 1)
                attention(b)
            pe.wait_ge(wT_ready, NB)
            ffn(NB - 1)

        @block.scalar
        def _(act):
            act.wait_ge(small_loaded, 16 * 7)
            act.wait_ge(consts, 1)
            act.wait_ge(prep_ps, 1)
            nc.scalar.activation(bk_rep[:, :], ones[:, :], ACT.Copy, scale=bqk[:, 1:2])
            nc.scalar.activation(gwT_s[:, :], SC[0][:, 2 * P:2 * P + NE], ACT.Copy)
            nc.scalar.activation(WqkT[:, :, :], SC[0][:, 0:2 * P].rearrange("p (a n) -> p a n", a=2), ACT.Copy
                                 ).then_inc(prep_act, 1)

            def yT(b):
                for h in range(NH):
                    act.wait_ge(yT_ps, NH * b + h + 1)
                    nc.scalar.activation(YT_h[:, h * HALF:(h + 1) * HALF], SC[h][:, :], ACT.Copy
                                         ).then_inc(yhi, 1)

            def keys(b):
                for h in range(NH):
                    act.wait_ge(kk_ps, NH * b + h + 1)
                    nc.scalar.activation(KK_h[:, h * HALF:(h + 1) * HALF], [TP, SC[0]][h][:, :], ACT.Identity,
                                         bias=wqbk[:, :]).then_inc(khi, 1)

            def exps(b, u):
                c0 = UNIT_COL[u]
                act.wait_ge(nb, NU * b + u + 1)
                nc.scalar.activation(E[:, UNIT_AT[u]:UNIT_AT[u] + HALF - c0], SC[u % 2][:, c0:HALF], ACT.Exp,
                                     bias=nbias[:, u:u + 1], scale=SCALE, accum_out=rsum[:, u:u + 1]
                                     ).then_inc(exps_done, 1)

            def factor(b):
                act.wait_ge(nmg_ready, b + 1)
                nc.scalar.activation(fac[:, :], val[:, :], ACT.Exp, bias=nmg[:, :]).then_inc(fexp, 1)

            def evacuate(b):
                for h in range(NH):
                    act.wait_ge(pv_ps, NH * b + h + 1)
                    nc.scalar.activation(OT[:, h * HALF:(h + 1) * HALF], SC[h][:, :], ACT.Copy
                                         ).then_inc(o_ev, 1)

            def ln_attention(b):
                act.wait_ge(nmr2, b + 1)
                for h in range(NH):
                    for t in range(TPH):
                        i = h * TPH + t
                        last = nc.scalar.activation(Y[:, i, :], [TP, SC[0]][h][:, t * P:(t + 1) * P], ACT.Identity,
                                                    bias=nmr[:, i:i + 1], scale=rs[:, i:i + 1])
                    last.then_inc(ox_ready, 1)

            def y2T(b, first):
                if not first:
                    act.wait_ge(u_ps, b * STEPS)
                for h in range(NH):
                    act.wait_ge(y2T_ps, NH * b + h + 1)
                    nc.scalar.activation(Y2_h[:, h * HALF:(h + 1) * HALF], [SC[1], TP][h][:, :], ACT.Copy
                                         ).then_inc(y2hi, 1)

            def gate(b):
                act.wait_ge(lg_ready, b + 1)
                nc.scalar.activation(eg[:, :, :], lg[:, :, :], ACT.Exp).then_inc(gexp, 1)

            def upper(b, k):
                r = rows(k % NC)
                act.wait_ge(h_ready, b * STEPS + k + 1)
                if k >= 3:
                    act.wait_ge(d_ps, b * STEPS + k - 2)
                nc.scalar.activation(H_h[0:r, k % 3, :], H[0:r, k % 2, :], ACT.Copy).then_inc(hi_ready, 1)

            def silu(b, k):
                r = rows(k % NC)
                act.wait_ge(g_ps, b * STEPS + k + 1)
                if k >= 2:
                    if (k - 2) % NC < NR:
                        act.wait_ge(u_used, b * ROUTED_STEPS + wb_count(k - 2))
                    else:
                        act.wait_ge(h_ready, b * STEPS + k - 1)
                nc.scalar.activation(S[0:r, k % 2, :], GB[0:r, :], ACT.Silu).then_inc(s_ready, 1)

            def ffn_evacuate(b, g):
                act.wait_ge(d_ps, b * STEPS + (g + 1) * NC)
                nc.scalar.activation(OF[:, :], DB[:, :], ACT.Copy).then_inc(fo_ev, 1)

            def ffn_ln(b, g):
                act.wait_ge(nmr4, NH * b + g + 1)
                for t in range(TPH):
                    last = nc.scalar.activation(FX[:, g, t, :], XB[:, t * P:(t + 1) * P], ACT.Identity,
                                                bias=fnmr[:, t:t + 1], scale=frs[:, t:t + 1])
                last.then_inc(fx_ready, 1)

            def ffn(b):
                for k in range(STEPS):
                    silu(b, k)
                    if k:
                        upper(b, k - 1)
                    if k == NC + 1:
                        ffn_evacuate(b, 0)
                    if k == NC + 5:
                        ffn_ln(b, 0)
                upper(b, STEPS - 1)
                ffn_evacuate(b, 1)
                ffn_ln(b, 1)

            def attention(b, first):
                yT(b)
                keys(b)
                for u in range(NU):
                    exps(b, u)
                factor(b)
                evacuate(b)
                ln_attention(b)
                y2T(b, first)
                gate(b)

            act.wait_ge(prep_dve, 1)
            attention(0, True)
            with act.Fori(1, NB) as b:
                ffn(b - 1)
                attention(b, False)
            ffn(NB - 1)

        @block.vector
        def _(dve):
            v = nc.vector
            DVE_STEPS = 42
            PREP = 11
            n = [0, 0]

            def step(ins):
                n[1] += 1
                ins.then_inc(dve_step, 1)
                dve.wait_ge(dve_step, n[0] * DVE_STEPS + n[1] + PREP)

            def begin(b):
                n[0], n[1] = b, 0

            m = [0]

            def prep(ins):
                m[0] += 1
                ins.then_inc(dve_step, 1)
                dve.wait_ge(dve_step, m[0])

            def normalise(b):
                for i in range(NT):
                    last = v.tensor_scalar(Y[:, i, :], X[:, b, i, :], mu[:, i:i + 1], rs[:, i:i + 1],
                                           ALU.subtract, ALU.mult)
                    yield i, last

            def merge(st, mu, dif, vs, ve, step):
                v.tensor_tensor(mu, st[:, :, 1], st[:, :, 4], ALU.add)
                v.tensor_tensor(dif, st[:, :, 1], st[:, :, 4], ALU.subtract)
                step(v.tensor_tensor(vs, st[:, :, 2], st[:, :, 5], ALU.add))
                v.tensor_scalar(mu, mu, 0.5, None, ALU.mult)
                step(v.scalar_tensor_tensor(dif, dif, 0.25, dif, ALU.mult, ALU.mult))
                step(v.scalar_tensor_tensor(ve, vs, 1.0 / D, dif, ALU.mult, ALU.add))

            def statistics(b, src):
                for i in range(NT):
                    last = v.bn_stats(st[:, i, :], src(i))
                step(last)
                merge(st, mu[:, :], dif[:, :], vs[:, :], ve[:, :], step)

            def ln1(b, x_count):
                dve.wait_ge(x_loaded, x_count)
                statistics(b, lambda i: X[:, b, i, :])
                v.tensor_scalar(ve[:, :], ve[:, :], EPS, None, ALU.add).then_inc(var1, 1)
                dve.wait_ge(pow1, b + 1)
                for i, last in normalise(b):
                    if i % TPH == TPH - 1:
                        last.then_inc(y_ready, 1)

            def yT(b):
                for h in range(NH):
                    c = slice(h * HALF, (h + 1) * HALF)
                    dve.wait_ge(yhi, NH * b + h + 1)
                    v.tensor_tensor(YT_l[:, c], SC[h][:, :], YT_h[:, c].bitcast(F32), ALU.subtract
                                    ).then_inc(ylo, 1)

            def keys(b):
                for h in range(NH):
                    c = slice(h * HALF, (h + 1) * HALF)
                    dve.wait_ge(khi, NH * b + h + 1)
                    v.scalar_tensor_tensor(KK_l[:, c], [TP, SC[0]][h][:, :], wqbk[:, :], KK_h[:, c].bitcast(F32),
                                           ALU.add, ALU.subtract).then_inc(klo, 1)

            def values(b):
                for h in range(NH):
                    dve.wait_ge(v_ps, NH * b + h + 1)
                    v.tensor_tensor(V[:, h * TPH:(h + 1) * TPH, :],
                                    [SC[1], TP][h][:, :].rearrange("p (t d) -> p t d", d=P),
                                    bv_b[:, None, :].to_broadcast([P, TPH, P]), ALU.add).then_inc(v_ev, 1)
                dve.wait_ge(c_ps, b + 1)
                v.tensor_scalar(cs[:, :], SC[0][:, 0:2 * NT].rearrange("p (t two) -> p t two", two=2)[:, :, 0],
                                bqbk[:, :], SCALE, ALU.add, ALU.mult).then_inc(c_ev, 1)

            def shift(b, u):
                dve.wait_ge(sc_ps, NU * b + u + 1)
                step(v.tensor_reduce(nmax[:, u:u + 1], SC[u % 2][:, UNIT_COL[u]:HALF], AX.X, ALU.max, negate=True))
                v.tensor_scalar(nbias[:, u:u + 1], nmax[:, u:u + 1], SCALE, None, ALU.mult).then_inc(nb, 1)

            def maximum(b):
                dve.wait_ge(nb, NU * (b + 1))
                v.tensor_tensor(val[:, 0:TPH], cs[:, 0:TPH], nbias[:, 0:TPH], ALU.subtract)
                step(v.tensor_tensor(val[:, TPH:NU], cs[:, :], nbias[:, TPH:NU], ALU.subtract))
                v.tensor_reduce(mx[:, :], val[:, :], AX.X, ALU.max).then_inc(mx_ready, 1)
                dve.wait_ge(maxT_ps, b + 1)
                v.tensor_reduce(m1[:, :], TP[0:1, 0:P], AX.X, ALU.max).then_inc(m1_ready, 1)
                dve.wait_ge(maxB_ps, b + 1)
                v.tensor_scalar(nmg[:, :], TP[:, P:P + 1], -1.0, None, ALU.mult).then_inc(nmg_ready, 1)

            def scale_values(b):
                dve.wait_ge(fexp, b + 1)
                dve.wait_ge(exps_done, NU * (b + 1))
                step(v.tensor_tensor(rf[:, :], rsum[:, :], fac[:, :], ALU.mult))
                v.tensor_reduce(zp[:, :], rf[:, :], AX.X, ALU.add).then_inc(zp_ready, 1)
                for h, (u0, k) in enumerate([(0, TPH), (TPH, NT)]):
                    v.tensor_tensor(VP[:, u0:u0 + k, :], V[:, 0:k, :],
                                    fac[:, u0:u0 + k, None].to_broadcast([P, k, P]), ALU.mult
                                    ).then_inc(vp_ready, 1)
                dve.wait_ge(z_ps, b + 1)
                step(v.tensor_copy(zs[:, :], TP[:, P:P + 1]))
                v.tensor_scalar(ez[:, :], zs[:, :], zs[:, :], EPS, ALU.mult, ALU.mult).then_inc(ez_ready, 1)

            def ln_attention(b):
                for h in range(NH):
                    dve.wait_ge(oT_ps, NH * b + h + 1)
                    for t in range(TPH):
                        last = v.bn_stats(st[:, h * TPH + t, :], [TP, SC[0]][h][:, t * P:(t + 1) * P])
                step(last)
                merge(st, mu[:, :], dif[:, :], vs[:, :], ve[:, :], step)
                dve.wait_ge(ez_ready, b + 1)
                v.tensor_scalar(ve[:, :], ve[:, :], ez[:, :], None, ALU.add).then_inc(var2, 1)
                dve.wait_ge(pow2, b + 1)
                v.scalar_tensor_tensor(nmr[:, :], mu[:, :], -1.0, rs[:, :], ALU.mult, ALU.mult
                                       ).then_inc(nmr2, 1)
                for h in range(NH):
                    dve.wait_ge(ox_ready, NH * b + h + 1)
                    for_half = X[:, b, h * TPH:(h + 1) * TPH, :]
                    last = v.tensor_tensor(for_half, for_half, Y[:, h * TPH:(h + 1) * TPH, :], ALU.add)
                step(last)
                v.memset(scratch[:, :], 0.0)

            def ln2(b):
                statistics(b, lambda i: X[:, b, i, :])
                v.tensor_scalar(ve[:, :], ve[:, :], EPS, None, ALU.add).then_inc(var3, 1)
                dve.wait_ge(pow3, b + 1)
                for i, last in normalise(b):
                    if i % TPH == TPH - 1:
                        last.then_inc(y2_ready, 1)

            def y2T(b):
                for h in range(NH):
                    c = slice(h * HALF, (h + 1) * HALF)
                    dve.wait_ge(y2hi, NH * b + h + 1)
                    v.tensor_tensor(Y2_l[:, c], [SC[1], TP][h][:, :], Y2_h[:, c].bitcast(F32), ALU.subtract
                                    ).then_inc(y2lo, 1)

            def gate(b, first):
                full = [P, NT, NE]
                dve.wait_ge(gate_ps, b + 1)
                logits = SC[0][:, 0:NT * NE].rearrange("p (t e) -> p t e", e=NE)
                step(v.tensor_reduce(gmax[:, :], logits, AX.X, ALU.max))
                v.tensor_tensor(lg[:, :, :], logits, gmax[:, :, None].to_broadcast(full), ALU.subtract
                                ).then_inc(lg_ready, 1)
                dve.wait_ge(gexp, b + 1)
                step(v.tensor_reduce(gsum[:, :], eg[:, :, :], AX.X, ALU.add))
                step(v.reciprocal(grec[:, :], gsum[:, :]))
                step(v.tensor_tensor(pg[:, :, :], eg[:, :, :], grec[:, :, None].to_broadcast(full), ALU.mult))
                cube = [P, NT, NE, NE]
                other = pg[:, :, None, :].to_broadcast(cube)
                own = pg[:, :, :, None].to_broadcast(cube)
                v.tensor_tensor(cmp_gt[:, :, :, :], other, own, ALU.is_gt)
                step(v.tensor_tensor(cmp_eq[:, :, :, :], other, own, ALU.is_equal))
                step(v.tensor_tensor(cmp_eq[:, :, :, :], cmp_eq[:, :, :, :],
                                     before[:, None, :, :].to_broadcast(cube), ALU.mult))
                step(v.tensor_tensor(cmp_gt[:, :, :, :], cmp_gt[:, :, :, :], cmp_eq[:, :, :, :], ALU.add))
                step(v.tensor_reduce(rank[:, :, :], cmp_gt[:, :, :, :], AX.X, ALU.add))
                step(v.scalar_tensor_tensor(wsel[:, :, :], rank[:, :, :], 2.0, pg[:, :, :], ALU.is_lt, ALU.mult))
                step(v.tensor_reduce(gsum[:, :], wsel[:, :, :], AX.X, ALU.add))
                step(v.tensor_scalar(gsum[:, :], gsum[:, :], 1e-20, None, ALU.add))
                step(v.reciprocal(grec[:, :], gsum[:, :]))
                step(v.tensor_tensor(wn[:, :, :], wsel[:, :, :], grec[:, :, None].to_broadcast(full), ALU.mult))
                step(v.tensor_copy(whl[:, :, 0, :], wn[:, :, :]))
                v.tensor_tensor(whl[:, :, 1, :], wn[:, :, :], whl[:, :, 0, :].bitcast(F32), ALU.subtract
                                ).then_inc(whl_ready, 1)
                if not first:
                    dve.wait_ge(wb_ps, b * ROUTED_STEPS)
                for h in range(NH):
                    dve.wait_ge(wT_ps, NH * b + h + 1)
                    last = v.tensor_copy(wT[:, h * HALF:(h + 1) * HALF], [SC[1], TP][h][0:2 * NE, :])
                last.then_inc(wT_ready, 1)

            def ffn_step(b, k):
                c, r = k % NC, rows(k % NC)
                dve.wait_ge(s_ready, b * STEPS + k + 1)
                dve.wait_ge(u_ps, b * STEPS + k + 1)
                sl = S[0:r, k % 2, :]
                if c < NR:
                    v.tensor_tensor(TU[0:r, k % 2, :], sl, UB[0:r, :], ALU.mult).then_inc(u_used, 1)
                    dve.wait_ge(u_used, b * ROUTED_STEPS + wb_count(k))
                    dve.wait_ge(wb_ps, b * ROUTED_STEPS + wb_count(k))
                if k >= 2:
                    dve.wait_ge(lo_ready, b * STEPS + k - 1)
                if c < NR:
                    last = v.tensor_tensor(H[0:r, k % 2, :], TU[0:r, k % 2, :], WB[0:r, :], ALU.mult)
                else:
                    last = v.tensor_tensor(H[0:r, k % 2, :], sl, UB[0:r, :], ALU.mult)
                last.then_inc(h_ready, 1)

            F_STEPS = 4 * NH

            def ffn_ln(b, g):
                f = [0]

                def fstep(ins):
                    f[0] += 1
                    ins.then_inc(f_step, 1)
                    dve.wait_ge(f_step, b * F_STEPS + g * 4 + f[0])

                dve.wait_ge(fT_ps, NH * b + g + 1)
                for t in range(TPH):
                    last = v.bn_stats(fst[:, t, :], XB[:, t * P:(t + 1) * P])
                fstep(last)
                merge(fst, fmu[:, :], fdif[:, :], fvs[:, :], fve[:, :], fstep)
                v.tensor_scalar(fve[:, :], fve[:, :], EPS, None, ALU.add).then_inc(var4, 1)

            def ffn_shift(b, g):
                dve.wait_ge(pow4, NH * b + g + 1)
                v.scalar_tensor_tensor(fnmr[:, :], fmu[:, :], -1.0, frs[:, :], ALU.mult, ALU.mult
                                       ).then_inc(nmr4, 1)

            def ffn_out(b, g):
                dve.wait_ge(fx_ready, NH * b + g + 1)
                xo = X[:, b, g * TPH:(g + 1) * TPH, :]
                v.tensor_tensor(xo, xo, FX[:, g, :, :], ALU.add).then_inc(out_ready, 1)

            def ffn(b):
                for k in range(STEPS):
                    ffn_step(b, k)
                    if k == NC + 3:
                        ffn_ln(b, 0)
                    if k == NC + 4:
                        ffn_shift(b, 0)
                    if k == NC + 6:
                        ffn_out(b, 0)
                ffn_ln(b, 1)
                ffn_shift(b, 1)
                ffn_out(b, 1)

            def attention(b, first):
                begin(b)
                ln1(b, 16 if first else 16 * NB)
                yT(b)
                keys(b)
                values(b)
                for u in range(NU):
                    shift(b, u)
                maximum(b)
                scale_values(b)
                ln_attention(b)
                ln2(b)
                y2T(b)
                gate(b, first)
                assert n[1] == DVE_STEPS, n[1]

            prep(v.memset(wkbq_s[:, :], 0.0))
            dve.wait_ge(small_loaded, 16 * 7)
            prep(v.tensor_copy(Wv_h[:, :], Wv_s[:, :]))
            prep(v.tensor_tensor(Wv_l[:, :], Wv_s[:, :], Wv_h[:, :].bitcast(F32), ALU.subtract))
            dve.wait_ge(prep_act, 1)
            prep(v.tensor_copy(gwT_h[:, :], gwT_s[:, :]))
            prep(v.tensor_tensor(gwT_l[:, :], gwT_s[:, :], gwT_h[:, :].bitcast(F32), ALU.subtract))
            dve.wait_ge(prep_ps, 2)
            prep(v.tensor_copy(A_h[:, :], SC[1][:, 0:P]))
            prep(v.tensor_tensor(A_l[:, :], SC[1][:, 0:P], A_h[:, :].bitcast(F32), ALU.subtract))
            prep(v.tensor_copy(wqbk[:, :], SC[1][:, P:P + 1]))
            prep(v.tensor_copy(wkbq_s[:, 0:1], SC[1][:, P + 1:P + 2]))
            prep(v.tensor_copy(bqbk[:, :], SC[1][:, P + 2:P + 3]))
            prep(v.tensor_copy(wkbq_h[:, :], wkbq_s[:, :]))
            v.tensor_tensor(wkbq_l[:, :], wkbq_s[:, :], wkbq_h[:, :].bitcast(F32), ALU.subtract
                            ).then_inc(prep_dve, 1)
            attention(0, True)
            with dve.Fori(1, NB) as b:
                ffn(b - 1)
                attention(b, False)
            ffn(NB - 1)


_INS = ["L0_attn_x", "L0_attn_Wq", "L0_attn_bq", "L0_attn_Wk", "L0_attn_bk", "L0_attn_Wv", "L0_attn_bv",
        "L0_ffn_gate_w", "L0_ffn_wg", "L0_ffn_wu", "L0_ffn_wd", "L0_ffn_swg", "L0_ffn_swu", "L0_ffn_swd"]


def kernel(**inputs):
    import concourse.bacc as _bacc
    from concourse.bass_utils import run_bass_kernel_spmd as _run

    nc = _bacc.Bacc("TRN2", target_bir_lowering=False, num_devices=1)
    arrays, args = {}, []
    for name in _INS:
        a = np.ascontiguousarray(inputs[name])
        arrays[f"in_{name}"] = a
        args.append(nc.dram_tensor(f"in_{name}", a.shape, mybir.dt.from_np(a.dtype), kind="ExternalInput").ap())
    args.append(nc.dram_tensor("out_0", (NB, T, D), F32, kind="ExternalOutput").ap())
    sandwich(nc, *args)
    r = _run(nc, [arrays], core_ids=[0])
    return r.results[0]["out_0"]
```

```python
from contextlib import ExitStack

import numpy as np

import concourse.bass as bass
from concourse import mybir

P = 128
NB, T, D = 4, 1024, 128
NT = T // P
HALF = 512
NH = T // HALF
TPH = HALF // P
NE, I, NS = 8, 176, 2
ROUTED, SHARED = NE * I, NS * I
FF = ROUTED + SHARED
NR = ROUTED // P
NC = -(-FF // P)
LASTC = FF - (NC - 1) * P
STEPS = NH * NC
ROUTED_STEPS = NH * NR
LAG_W, LAG_H, LAG_D = 1, 2, 3
RING = 4
EPS = 1e-5
SCALE = float(D) ** -0.5
NEG = -1e30

UNITS = [(h, j) for h in range(NH) for j in range(TPH * (h + 1))]
NU = len(UNITS)
UNIT_COL = [max(0, P * j - HALF * h) for h, j in UNITS]
UNIT_AT = [sum(HALF - c for c in UNIT_COL[:u]) for u in range(NU)]
E_COLS = sum(HALF - c for c in UNIT_COL)

F32 = mybir.dt.float32
F32R = mybir.dt.float32r
BF16 = mybir.dt.bfloat16
ALU = mybir.AluOpType
ACT = mybir.ActivationFunctionType
AX = mybir.AxisListType


def rows(c):
    return LASTC if c == NC - 1 else P


def wb_count(k):
    return (k // NC) * NR + min(k % NC + 1, NR)


def sandwich(nc, x, Wq, bq, Wk, bk, Wv, bv, gate_w, wg, wu, wd, swg, swu, swd, out):
    ctx = ExitStack()
    with ctx:
        def sb(name, shape, dt=F32):
            return ctx.enter_context(nc.sbuf_tensor(name, shape, dt))

        def sem(name):
            return ctx.enter_context(nc.semaphore(name))

        ident = sb("ident", [P, P])
        identb = sb("identb", [P, P], BF16)
        ones = sb("ones", [P, P])
        maskb = sb("maskb", [P, P], BF16)
        before = sb("before", [P, NE, NE])
        neg_half = sb("neg_half", [P, NT])
        sel_two = sb("sel_two", [2 * NE, 2, ROUTED], BF16)
        sel = sb("sel", [2 * NE, ROUTED], F32R)
        Wqk_s = sb("Wqk_s", [P, 2, P])
        WqkT = sb("WqkT", [P, 2, P])
        Wv_s = sb("Wv_s", [P, P])
        bqk = sb("bqk", [P, 2])
        bk_rep = sb("bk_rep", [P, P])
        bv_b = sb("bv_b", [P, P])
        gw_s = sb("gw_s", [NE, P])
        A_h, A_l = sb("A_h", [P, P], F32R), sb("A_l", [P, P], F32R)
        Wv_h, Wv_l = sb("Wv_h", [P, P], F32R), sb("Wv_l", [P, P], F32R)
        wkbq_s = sb("wkbq_s", [P, 2])
        wkbq_h, wkbq_l = sb("wkbq_h", [P, 2], F32R), sb("wkbq_l", [P, 2], F32R)
        wqbk = sb("wqbk", [P, 1])
        bqbk = sb("bqbk", [P, 1])
        gwT_s = sb("gwT_s", [P, NE])
        gwT_h, gwT_l = sb("gwT_h", [P, NE], F32R), sb("gwT_l", [P, NE], F32R)
        Wg_s, Wu_s, Wd_s = sb("Wg_s", [P, FF]), sb("Wu_s", [P, FF]), sb("Wd_s", [P, NC, P])
        Wg_h, Wg_l = sb("Wg_h", [P, FF], F32R), sb("Wg_l", [P, FF], F32R)
        Wu_h, Wu_l = sb("Wu_h", [P, FF], F32R), sb("Wu_l", [P, FF], F32R)
        Wd_h, Wd_l = sb("Wd_h", [P, NC, P], F32R), sb("Wd_l", [P, NC, P], F32R)

        X = sb("X", [P, NB, NT, P])
        Y = sb("Y", [P, NT, P])
        YT_h, YT_l = sb("YT_h", [P, T], F32R), sb("YT_l", [P, T], F32R)
        KK_h, KK_l = sb("KK_h", [P, T], F32R), sb("KK_l", [P, T], F32R)
        V = sb("V", [P, NT, P])
        VP = sb("VP", [P, NU, P])
        E = sb("E", [P, E_COLS])
        OT = sb("OT", [P, T])
        Y2_h, Y2_l = sb("Y2_h", [P, T], F32R), sb("Y2_l", [P, T], F32R)
        st = sb("st", [P, NT, 6])
        mu, dif, vs = sb("mu", [P, NT]), sb("dif", [P, NT]), sb("vs", [P, NT])
        ve = sb("ve", [P, NT])
        rs = sb("rs", [P, NT])
        nmr = sb("nmr", [P, NT])
        nmax = sb("nmax", [P, NU])
        nbias = sb("nbias", [P, NU])
        rsum = sb("rsum", [P, NU])
        cs = sb("cs", [P, NT])
        val = sb("val", [P, NU])
        mx = sb("mx", [P, 1])
        m1 = sb("m1", [1, 1])
        nmg = sb("nmg", [P, 1])
        fac = sb("fac", [P, NU])
        rf = sb("rf", [P, NU])
        zp = sb("zp", [P, 1])
        zs = sb("zs", [P, 1])
        ez = sb("ez", [P, 1])
        gmax = sb("gmax", [P, NT])
        lg = sb("lg", [P, NT, NE])
        eg = sb("eg", [P, NT, NE])
        gsum = sb("gsum", [P, NT])
        grec = sb("grec", [P, NT])
        pg = sb("pg", [P, NT, NE])
        cmp_gt = sb("cmp_gt", [P, NT, NE, NE])
        cmp_eq = sb("cmp_eq", [P, NT, NE, NE])
        rank = sb("rank", [P, NT, NE])
        wsel = sb("wsel", [P, NT, NE])
        wn = sb("wn", [P, NT, NE])
        whl = sb("whl", [P, NT, 2, NE], F32R)
        wT = sb("wT", [2 * NE, T], F32R)
        wT_next = sb("wT_next", [2 * NE, HALF], F32R)
        S = sb("S", [P, 2, HALF])
        TU = sb("TU", [P, 2, HALF])
        H = sb("H", [P, RING, HALF])
        H_h, H_l = sb("H_h", [P, RING, HALF], F32R), sb("H_l", [P, RING, HALF], F32R)
        OF = sb("OF", [P, HALF])
        fst = sb("fst", [P, TPH, 6])
        fmu, fdif, fvs = sb("fmu", [P, TPH]), sb("fdif", [P, TPH]), sb("fvs", [P, TPH])
        fve = sb("fve", [P, TPH])
        frs = sb("frs", [P, TPH])
        fnmr = sb("fnmr", [P, TPH])
        FX = sb("FX", [P, TPH, P])

        def bank(name):
            return ctx.enter_context(nc.psum_tensor(name, [P, HALF], F32))

        SC = [bank("SC0"), bank("SC1")]
        GB, UB = [bank("GB0"), bank("GB1")], [bank("UB0"), bank("UB1")]
        WB, DB = bank("WB"), bank("DB")

        x_loaded = sem("x_loaded")
        small_loaded = sem("small_loaded")
        wg_loaded = sem("wg_loaded")
        wu_loaded = sem("wu_loaded")
        wd_loaded = sem("wd_loaded")
        out_stored = sem("out_stored")
        consts = sem("consts")
        pool_step = sem("pool_step")
        prep_ps = sem("prep_ps")
        prep_act = sem("prep_act")
        prep_dve = sem("prep_dve")
        wgu_split = sem("wgu_split")
        wd_split = sem("wd_split")
        var1 = sem("var1")
        pow1 = sem("pow1")
        y_ready = sem("y_ready")
        yT_ps = sem("yT_ps")
        yhi = sem("yhi")
        ylo = sem("ylo")
        kk_ps = sem("kk_ps")
        khi = sem("khi")
        klo = sem("klo")
        v_ps = sem("v_ps")
        v_ev = sem("v_ev")
        c_ps = sem("c_ps")
        c_ev = sem("c_ev")
        sc_ps = sem("sc_ps")
        nb = sem("nb")
        exps_done = sem("exps_done")
        mx_ready = sem("mx_ready")
        maxT_ps = sem("maxT_ps")
        m1_ready = sem("m1_ready")
        maxB_ps = sem("maxB_ps")
        nmg_ready = sem("nmg_ready")
        fexp = sem("fexp")
        zp_ready = sem("zp_ready")
        z_ps = sem("z_ps")
        vp_ready = sem("vp_ready")
        ez_ready = sem("ez_ready")
        pv_ps = sem("pv_ps")
        o_ev = sem("o_ev")
        oT_ps = sem("oT_ps")
        var2 = sem("var2")
        pow2 = sem("pow2")
        nmr2 = sem("nmr2")
        ox_ready = sem("ox_ready")
        x1_ready = sem("x1_ready")
        var3 = sem("var3")
        pow3 = sem("pow3")
        y2_ready = sem("y2_ready")
        y2T_ps = sem("y2T_ps")
        y2hi = sem("y2hi")
        y2lo = sem("y2lo")
        gate_ps = sem("gate_ps")
        lg_ready = sem("lg_ready")
        gexp = sem("gexp")
        whl_ready = sem("whl_ready")
        wT_ps = sem("wT_ps")
        wT_ready = sem("wT_ready")
        y2_moved = sem("y2_moved")
        wT_moved = sem("wT_moved")
        g_ps = sem("g_ps")
        u_ps = sem("u_ps")
        wb_ps = sem("wb_ps")
        d_ps = sem("d_ps")
        s_ready = sem("s_ready")
        u_used = sem("u_used")
        h_ready = sem("h_ready")
        hi_ready = sem("hi_ready")
        lo_ready = sem("lo_ready")
        fo_ev = sem("fo_ev")
        f_step = sem("f_step")
        fT_ps = sem("fT_ps")
        var4 = sem("var4")
        pow4 = sem("pow4")
        nmr4 = sem("nmr4")
        fx_ready = sem("fx_ready")
        out_ready = sem("out_ready")
        dve_step = sem("dve_step")

        def split3(pe, out_ap, wh, wl, xh, xl):
            nc.tensor.matmul(out_ap, wh, xh, start=True, stop=False)
            nc.tensor.matmul(out_ap, wh, xl, start=False, stop=False)
            return nc.tensor.matmul(out_ap, wl, xh, start=False, stop=True)

        block = ctx.enter_context(nc.Block())

        @block.sync
        def _(sp):
            xt = x.rearrange("b (t p) d -> b p t d", p=P)
            ot = out.rearrange("b (g t p) d -> b g p t d", g=NH, p=P)
            sp.dma_start(X[:, 0, :, :], xt[0]).then_inc(x_loaded, 16)
            sp.dma_start(Wqk_s[:, 0, :], Wq).then_inc(small_loaded, 16)
            sp.dma_start(Wqk_s[:, 1, :], Wk).then_inc(small_loaded, 16)
            sp.dma_start(bqk[:, 0:1], bq.rearrange("(p o) -> p o", o=1)).then_inc(small_loaded, 16)
            sp.dma_start(bqk[:, 1:2], bk.rearrange("(p o) -> p o", o=1)).then_inc(small_loaded, 16)
            sp.dma_start(gw_s[:, :], gate_w).then_inc(small_loaded, 16)
            sp.dma_start(Wv_s[:, :], Wv).then_inc(small_loaded, 16)
            sp.dma_start(bv_b[:, :], bv.rearrange("(o d) -> o d", o=1).to_broadcast([P, P])
                         ).then_inc(small_loaded, 16)
            rt = slice(0, ROUTED)
            sh = slice(ROUTED, FF)
            sp.dma_start(Wg_s[:, rt].rearrange("p (e i) -> p e i", e=NE),
                         wg.rearrange("e h i -> h e i")).then_inc(wg_loaded, 16)
            sp.dma_start(Wg_s[:, sh], swg).then_inc(wg_loaded, 16)
            sp.dma_start(Wu_s[:, rt].rearrange("p (e i) -> p e i", e=NE),
                         wu.rearrange("e h i -> h e i")).then_inc(wu_loaded, 16)
            sp.dma_start(Wu_s[:, sh], swu).then_inc(wu_loaded, 16)
            sp.dma_start(Wd_s[:, 0:NR, :], wd.rearrange("e i h -> (e i) h").rearrange("(c p) h -> p c h", p=P)
                         ).then_inc(wd_loaded, 16)
            full = NC - 1 - NR
            sp.dma_start(Wd_s[:, NR:NC - 1, :], swd[0:full * P, :].rearrange("(c p) h -> p c h", p=P)
                         ).then_inc(wd_loaded, 16)
            sp.dma_start(Wd_s[0:LASTC, NC - 1, :], swd[full * P:SHARED, :]).then_inc(wd_loaded, 16)
            for b in range(1, NB):
                sp.wait_ge(x_loaded, 16 * b)
                sp.dma_start(X[:, b, :, :], xt[b]).then_inc(x_loaded, 16)
            for b in range(NB):
                for g in range(NH):
                    sp.wait_ge(out_ready, NH * b + g + 1)
                    sp.dma_start(ot[b, g], X[:, b, g * TPH:(g + 1) * TPH, :]).then_inc(out_stored, 16)
            sp.wait_ge(out_stored, 16 * NB * NH)

        @block.gpsimd
        def _(pool):
            n = [0]

            def step(ins):
                n[0] += 1
                ins.then_inc(pool_step, 1)
                pool.wait_ge(pool_step, n[0])

            step(nc.gpsimd.memset(ident[:, :], 0.0))
            step(nc.gpsimd.affine_select(out=ident[:, :], in_=ident[:, :], compare_op=ALU.not_equal, fill=1.0,
                                         base=0, pattern=[[-1, P]], channel_multiplier=1))
            nc.gpsimd.memset(neg_half[:, :], -0.5)
            nc.gpsimd.memset(ones[:, :], 1.0)
            step(nc.gpsimd.memset(maskb[:, :], 0.0))
            step(nc.gpsimd.affine_select(out=maskb[:, :], in_=maskb[:, :], compare_op=ALU.is_ge, fill=NEG,
                                         base=0, pattern=[[1, P]], channel_multiplier=-1))
            nc.gpsimd.tensor_copy(identb[:, :], ident[:, :]).then_inc(consts, 1)

            def power(dst, src, width):
                return nc.gpsimd.tensor_tensor(dst, src, neg_half[:, 0:width], ALU.pow)

            def pow_ln1(b):
                pool.wait_ge(var1, b + 1)
                power(rs[:, :], ve[:, :], NT).then_inc(pow1, 1)

            def pow_attention(b):
                pool.wait_ge(var2, b + 1)
                power(rs[:, :], ve[:, :], NT).then_inc(pow2, 1)

            def pow_ln2(b):
                pool.wait_ge(var3, b + 1)
                power(rs[:, :], ve[:, :], NT).then_inc(pow3, 1)

            pow_ln1(0)
            step(nc.gpsimd.memset(before[:, :, :], 1.0))
            step(nc.gpsimd.affine_select(out=before[:, :, :], in_=before[:, :, :], compare_op=ALU.is_ge, fill=0.0,
                                         base=-1, pattern=[[1, NE], [-1, NE]], channel_multiplier=0))
            step(nc.gpsimd.memset(sel_two[:, :, :], 1.0))
            step(nc.gpsimd.affine_select(out=sel_two[:, :, :], in_=sel_two[:, :, :], compare_op=ALU.is_ge, fill=0.0,
                                         base=0, pattern=[[ROUTED, 2], [1, ROUTED]], channel_multiplier=-I))
            step(nc.gpsimd.affine_select(out=sel_two[:, :, :], in_=sel_two[:, :, :], compare_op=ALU.is_ge, fill=0.0,
                                         base=I - 1, pattern=[[-ROUTED, 2], [-1, ROUTED]], channel_multiplier=I))
            nc.gpsimd.tensor_tensor(sel[:, :], sel_two[:, 0, :], sel_two[:, 1, :], ALU.add
                                    ).then_inc(consts, 1)

            def split(hi, lo, src):
                step(nc.gpsimd.tensor_copy(hi, src))
                return nc.gpsimd.tensor_tensor(lo, src, hi.bitcast(F32), ALU.subtract)

            pool.wait_ge(wg_loaded, 32)
            split(Wg_h[:, :], Wg_l[:, :], Wg_s[:, :]).then_inc(wgu_split, 1)
            pool.wait_ge(wu_loaded, 32)
            split(Wu_h[:, :], Wu_l[:, :], Wu_s[:, :]).then_inc(wgu_split, 1)
            pow_attention(0)
            pow_ln2(0)
            pool.wait_ge(wd_loaded, 48)
            split(Wd_h[:, 0:NC - 1, :], Wd_l[:, 0:NC - 1, :], Wd_s[:, 0:NC - 1, :])
            split(Wd_h[0:LASTC, NC - 1, :], Wd_l[0:LASTC, NC - 1, :], Wd_s[0:LASTC, NC - 1, :]
                  ).then_inc(wd_split, 1)

            def lower(f, k, first):
                r = rows(k % NC)
                pool.wait_ge(h_ready, f * STEPS + k + 1)
                pool.wait_ge(hi_ready, f * STEPS + k + 1)
                if k >= RING or not first:
                    pool.wait_ge(d_ps, f * STEPS + k + 1 - RING)
                q = k % RING
                nc.gpsimd.tensor_tensor(H_l[0:r, q, :], H[0:r, q, :], H_h[0:r, q, :].bitcast(F32),
                                        ALU.subtract).then_inc(lo_ready, 1)

            def ffn_pow(f, g):
                pool.wait_ge(var4, NH * f + g + 1)
                power(frs[:, :], fve[:, :], TPH).then_inc(pow4, 1)

            def body(b, first, last=False):
                f = b - 1
                for k in range(STEPS):
                    if k >= LAG_H:
                        lower(f, k - LAG_H, first)
                    elif not first:
                        lower(f - 1, STEPS + k - LAG_H, False)
                    if k == 1 and not last:
                        pow_ln1(b)
                    if k == 5 and not first:
                        ffn_pow(f - 1, 1)
                    if k == 16 and not last:
                        pow_attention(b)
                    if k == 20 and not last:
                        pow_ln2(b)
                    if k == 20:
                        ffn_pow(f, 0)

            body(1, True)
            with pool.Fori(2, NB) as b:
                body(b, False)
            body(NB, False, last=True)
            for k in range(STEPS - LAG_H, STEPS):
                lower(NB - 1, k, False)
            ffn_pow(NB - 1, 1)

        @block.tensor
        def _(pe):
            pe.wait_ge(consts, 1)
            pe.wait_ge(small_loaded, 16 * 7)
            nc.tensor.transpose(SC[0][:, 0:P], Wqk_s[:, 0, :], ident[:, :])
            nc.tensor.transpose(SC[0][:, P:2 * P], Wqk_s[:, 1, :], ident[:, :])
            nc.tensor.transpose(SC[0][:, 2 * P:2 * P + NE], gw_s[:, :], ident[0:NE, 0:NE]
                                ).then_inc(prep_ps, 1)
            pe.wait_ge(prep_act, 1)
            nc.tensor.matmul(SC[1][:, 0:P], WqkT[:, 1, :], WqkT[:, 0, :], start=True, stop=True)
            nc.tensor.matmul(SC[1][:, P:P + 1], WqkT[:, 0, :], bqk[:, 1:2], start=True, stop=True)
            nc.tensor.matmul(SC[1][:, P + 1:P + 2], WqkT[:, 1, :], bqk[:, 0:1], start=True, stop=True)
            nc.tensor.matmul(SC[1][:, P + 2:P + 3], bk_rep[:, :], bqk[:, 0:1], start=True, stop=True
                             ).then_inc(prep_ps, 1)

            def transposes(dst, src):
                for t in range(TPH):
                    last = nc.tensor.transpose(dst[:, t * P:(t + 1) * P], src(t), ident[:, :])
                return last

            def yT(b, h, first=True):
                if h == 1 and not first:
                    pe.wait_ge(fx_ready, NH * (b - 1))
                pe.wait_ge(y_ready, NH * b + h + 1)
                transposes(SC[h], lambda t: Y[:, h * TPH + t, :]).then_inc(yT_ps, 1)

            def keys(b, h):
                c = slice(h * HALF, (h + 1) * HALF)
                pe.wait_ge(ylo, NH * b + h + 1)
                split3(pe, SC[h][:, :], A_h[:, :], A_l[:, :], YT_h[:, c], YT_l[:, c]).then_inc(kk_ps, 1)

            def values(b, h):
                pe.wait_ge(klo, NH * b + h + 1)
                for t in range(TPH):
                    c = slice((h * TPH + t) * P, (h * TPH + t + 1) * P)
                    last = split3(pe, SC[h][:, t * P:(t + 1) * P], YT_h[:, c], YT_l[:, c], Wv_h[:, :], Wv_l[:, :])
                last.then_inc(v_ps, 1)

            def key_terms(b):
                pe.wait_ge(v_ev, NH * b + 1)
                for t in range(NT):
                    c = slice(t * P, (t + 1) * P)
                    last = split3(pe, SC[0][:, 2 * t:2 * t + 2], YT_h[:, c], YT_l[:, c],
                                  wkbq_h[:, :], wkbq_l[:, :])
                last.then_inc(c_ps, 1)

            def scores(b, u):
                h, j = UNITS[u]
                c0 = UNIT_COL[u]
                if u == 0:
                    pe.wait_ge(c_ev, b + 1)
                elif u == 1:
                    pe.wait_ge(v_ev, NH * (b + 1))
                else:
                    pe.wait_ge(exps_done, NU * b + u - 1)
                dst = SC[u % 2][:, c0:HALF]
                q = slice(h * HALF + c0, (h + 1) * HALF)
                kt = slice(j * P, (j + 1) * P)
                diag = j * P >= h * HALF
                nc.tensor.matmul(dst, KK_h[:, kt], YT_h[:, q], start=True, stop=False)
                nc.tensor.matmul(dst, KK_h[:, kt], YT_l[:, q], start=False, stop=False)
                last = nc.tensor.matmul(dst, KK_l[:, kt], YT_h[:, q], start=False, stop=not diag)
                if diag:
                    last = nc.tensor.matmul(SC[u % 2][:, c0:c0 + P], identb[:, :], maskb[:, :],
                                            start=False, stop=True)
                last.then_inc(sc_ps, 1)

            def max_row(b):
                pe.wait_ge(exps_done, NU * (b + 1))
                pe.wait_ge(mx_ready, b + 1)
                nc.tensor.transpose(SC[0][0:1, 0:P], mx[:, :], ident[:, :]).then_inc(maxT_ps, 1)

            def max_all(b):
                pe.wait_ge(m1_ready, b + 1)
                nc.tensor.matmul(SC[0][:, P:P + 1], ones[0:1, :], m1[:, :], start=True, stop=True
                                 ).then_inc(maxB_ps, 1)

            def sum_all(b):
                pe.wait_ge(zp_ready, b + 1)
                nc.tensor.matmul(SC[0][:, P:P + 1], ones[:, :], zp[:, :], start=True, stop=True
                                 ).then_inc(z_ps, 1)

            def attend(b, h, j0, j1):
                pe.wait_ge(vp_ready, NH * b + h + 1)
                if h == 1:
                    pe.wait_ge(ez_ready, b + 1)
                end = TPH * (h + 1)
                for j in range(j0, j1):
                    u = UNITS.index((h, j))
                    c0 = UNIT_COL[u]
                    last = nc.tensor.matmul(SC[1 - h][:, c0:HALF], VP[:, u, :],
                                            E[:, UNIT_AT[u]:UNIT_AT[u] + HALF - c0], start=j == 0, stop=j == end - 1)
                if j1 == end:
                    last.then_inc(pv_ps, 1)

            def oT(b, h):
                pe.wait_ge(o_ev, NH * b + h + 1)
                transposes(SC[1 - h], lambda t: OT[:, (h * TPH + t) * P:(h * TPH + t + 1) * P]).then_inc(oT_ps, 1)

            def y2T(b, h, alone=False):
                if h == 1 and not alone:
                    pe.wait_ge(fx_ready, NH * (b - 1) + 1)
                pe.wait_ge(y2_ready, NH * b + h + 1)
                transposes(SC[h], lambda t: Y[:, h * TPH + t, :]).then_inc(y2T_ps, 1)

            def gate(b):
                pe.wait_ge(y2lo, NH * (b + 1))
                for t in range(NT):
                    yh, yl = (Y2_h, Y2_l) if t < TPH else (YT_h, YT_l)
                    c = slice(t * P, (t + 1) * P)
                    last = split3(pe, SC[0][:, NE * t:NE * (t + 1)], yh[:, c], yl[:, c], gwT_h[:, :], gwT_l[:, :])
                last.then_inc(gate_ps, 1)

            def weightsT(b):
                pe.wait_ge(whl_ready, b + 1)
                for h in range(NH):
                    for t in range(TPH):
                        last = nc.tensor.transpose(SC[1 - h][0:2 * NE, t * P:(t + 1) * P],
                                                   whl[:, h * TPH + t, :, :].rearrange("p a e -> p (a e)").bitcast(F32),
                                                   ident[:, :])
                    last.then_inc(wT_ps, 1)

            def projections(f, k, first):
                g, c = divmod(k, NC)
                r = rows(c)
                ic = slice(c * P, c * P + r)
                tok = slice(g * HALF, (g + 1) * HALF)
                if k == 0:
                    pe.wait_ge(y2lo, NH * f + 1)
                if k == NC:
                    pe.wait_ge(y2_moved, f + 1)
                if k >= 2 or not first:
                    pe.wait_ge(s_ready, f * STEPS + k - 1)
                split3(pe, GB[k % 2][0:r, :], Wg_h[:, ic], Wg_l[:, ic], Y2_h[:, tok], Y2_l[:, tok]).then_inc(g_ps, 1)
                if k >= 2 and (k - 2) % NC < NR:
                    pe.wait_ge(u_used, f * ROUTED_STEPS + wb_count(k - 2))
                elif k >= 2 or not first:
                    pe.wait_ge(h_ready, f * STEPS + k - 1)
                split3(pe, UB[k % 2][0:r, :], Wu_h[:, ic], Wu_l[:, ic], Y2_h[:, tok], Y2_l[:, tok]).then_inc(u_ps, 1)

            def weights(f, k, first):
                g, c = divmod(k, NC)
                if c >= NR:
                    return
                if k == 0:
                    pe.wait_ge(wT_ready, f + 1)
                if k == NC:
                    pe.wait_ge(wT_moved, f + 1)
                if k > 0 or not first:
                    before_it = k if c else k - (NC - NR)
                    pe.wait_ge(h_ready, f * STEPS + before_it)
                nc.tensor.matmul(WB[:, :], sel[:, c * P:(c + 1) * P], wT[:, g * HALF:(g + 1) * HALF],
                                 start=True, stop=True).then_inc(wb_ps, 1)

            def down(f, k, first):
                c, r = k % NC, rows(k % NC)
                if c == 0 and (k > 0 or not first):
                    pe.wait_ge(fo_ev, NH * f + k // NC)
                pe.wait_ge(lo_ready, f * STEPS + k + 1)
                for i, (w, hh) in enumerate([(Wd_h, H_h), (Wd_h, H_l), (Wd_l, H_h)]):
                    last = nc.tensor.matmul(DB[:, :], w[0:r, c, :], hh[0:r, k % RING, :],
                                            start=c == 0 and i == 0, stop=c == NC - 1 and i == 2)
                last.then_inc(d_ps, 1)

            def fT(f, g, b=None):
                if b is not None:
                    pe.wait_ge(ox_ready, NH * b + 1)
                pe.wait_ge(fo_ev, NH * f + g + 1)
                transposes(SC[1], lambda t: OF[:, t * P:(t + 1) * P]).then_inc(fT_ps, 1)

            def body(b, first, last=False):
                f = b - 1
                for k in range(STEPS):
                    projections(f, k, first)
                    if k == 11 and not last:
                        max_row(b)
                    if k >= LAG_W:
                        weights(f, k - LAG_W, first)
                    if k == 11 and not last:
                        max_all(b)
                    if k >= LAG_D:
                        down(f, k - LAG_D, first)
                    elif not first:
                        down(f - 1, STEPS + k - LAG_D, False)
                    if k == 4 and not first:
                        fT(f - 1, 1)
                    if k == 19:
                        fT(f, 0, None if last else b)
                    if last:
                        continue
                    if k == 3:
                        yT(b, 0)
                    if k == 5:
                        keys(b, 0)
                    if k == 6:
                        values(b, 0)
                        yT(b, 1, first)
                    if k == 8:
                        keys(b, 1)
                        key_terms(b)
                    if k == 9:
                        values(b, 1)
                    if k == 10:
                        for u in range(NU):
                            scores(b, u)
                    if k == 12:
                        sum_all(b)
                        attend(b, 0, 0, TPH)
                    if k == 13:
                        attend(b, 1, 0, TPH)
                    if k == 14:
                        attend(b, 1, TPH, NT)
                        oT(b, 0)
                    if k == 15:
                        oT(b, 1)
                    if k == 22:
                        y2T(b, 0)
                    if k == 23:
                        y2T(b, 1)
                    if k == 25:
                        gate(b)
                if not last:
                    weightsT(b)

            pe.wait_ge(prep_dve, 1)
            yT(0, 0)
            yT(0, 1)
            keys(0, 0)
            keys(0, 1)
            values(0, 0)
            values(0, 1)
            key_terms(0)
            for u in range(NU):
                scores(0, u)
            max_row(0)
            max_all(0)
            sum_all(0)
            attend(0, 0, 0, TPH)
            attend(0, 1, 0, NT)
            oT(0, 0)
            oT(0, 1)
            y2T(0, 0)
            y2T(0, 1, alone=True)
            gate(0)
            weightsT(0)
            pe.wait_ge(wgu_split, 2)
            pe.wait_ge(consts, 2)
            pe.wait_ge(wd_split, 1)
            body(1, True)
            with pe.Fori(2, NB) as b:
                body(b, False)
            body(NB, False, last=True)
            for k in range(STEPS - LAG_D, STEPS):
                down(NB - 1, k, False)
            fT(NB - 1, 1)

        @block.scalar
        def _(act):
            act.wait_ge(small_loaded, 16 * 7)
            act.wait_ge(consts, 1)
            act.wait_ge(prep_ps, 1)
            nc.scalar.activation(bk_rep[:, :], ones[:, :], ACT.Copy, scale=bqk[:, 1:2])
            nc.scalar.activation(gwT_s[:, :], SC[0][:, 2 * P:2 * P + NE], ACT.Copy)
            nc.scalar.activation(WqkT[:, :, :], SC[0][:, 0:2 * P].rearrange("p (a n) -> p a n", a=2), ACT.Copy
                                 ).then_inc(prep_act, 1)

            def yT(b, h):
                act.wait_ge(yT_ps, NH * b + h + 1)
                nc.scalar.activation(YT_h[:, h * HALF:(h + 1) * HALF], SC[h][:, :], ACT.Copy).then_inc(yhi, 1)

            def keys(b, h):
                act.wait_ge(kk_ps, NH * b + h + 1)
                nc.scalar.activation(KK_h[:, h * HALF:(h + 1) * HALF], SC[h][:, :], ACT.Identity,
                                     bias=wqbk[:, :]).then_inc(khi, 1)

            def exps(b, u):
                c0 = UNIT_COL[u]
                act.wait_ge(nb, NU * b + u + 1)
                nc.scalar.activation(E[:, UNIT_AT[u]:UNIT_AT[u] + HALF - c0], SC[u % 2][:, c0:HALF], ACT.Exp,
                                     bias=nbias[:, u:u + 1], scale=SCALE, accum_out=rsum[:, u:u + 1]
                                     ).then_inc(exps_done, 1)

            def factor(b):
                act.wait_ge(nmg_ready, b + 1)
                nc.scalar.activation(fac[:, :], val[:, :], ACT.Exp, bias=nmg[:, :]).then_inc(fexp, 1)

            def evacuate(b, h):
                act.wait_ge(pv_ps, NH * b + h + 1)
                nc.scalar.activation(OT[:, h * HALF:(h + 1) * HALF], SC[1 - h][:, :], ACT.Copy).then_inc(o_ev, 1)

            def ln_attention(b, h):
                act.wait_ge(nmr2, b + 1)
                for t in range(TPH):
                    i = h * TPH + t
                    last = nc.scalar.activation(Y[:, i, :], SC[1 - h][:, t * P:(t + 1) * P], ACT.Identity,
                                                bias=nmr[:, i:i + 1], scale=rs[:, i:i + 1])
                last.then_inc(ox_ready, 1)

            def y2T(b, h, alone=False):
                if h == 0 and not alone:
                    act.wait_ge(u_ps, (b - 1) * STEPS + NC)
                act.wait_ge(y2T_ps, NH * b + h + 1)
                dst = [Y2_h, YT_h][h]
                nc.scalar.activation(dst[:, h * HALF:(h + 1) * HALF], SC[h][:, :], ACT.Copy).then_inc(y2hi, 1)

            def gate(b):
                act.wait_ge(lg_ready, b + 1)
                nc.scalar.activation(eg[:, :, :], lg[:, :, :], ACT.Exp).then_inc(gexp, 1)

            def upper(f, k, first):
                r = rows(k % NC)
                act.wait_ge(h_ready, f * STEPS + k + 1)
                if k >= RING or not first:
                    act.wait_ge(d_ps, f * STEPS + k + 1 - RING)
                nc.scalar.activation(H_h[0:r, k % RING, :], H[0:r, k % RING, :], ACT.Copy).then_inc(hi_ready, 1)

            def silu(f, k, first):
                r = rows(k % NC)
                act.wait_ge(g_ps, f * STEPS + k + 1)
                if k >= 2 and (k - 2) % NC < NR:
                    act.wait_ge(u_used, f * ROUTED_STEPS + wb_count(k - 2))
                elif k >= 2 or not first:
                    act.wait_ge(h_ready, f * STEPS + k - 1)
                nc.scalar.activation(S[0:r, k % 2, :], GB[k % 2][0:r, :], ACT.Silu).then_inc(s_ready, 1)

            def ffn_evacuate(f, g):
                act.wait_ge(d_ps, f * STEPS + (g + 1) * NC)
                nc.scalar.activation(OF[:, :], DB[:, :], ACT.Copy).then_inc(fo_ev, 1)

            def ffn_ln(f, g):
                act.wait_ge(nmr4, NH * f + g + 1)
                for t in range(TPH):
                    last = nc.scalar.activation(FX[:, t, :], SC[1][:, t * P:(t + 1) * P], ACT.Identity,
                                                bias=fnmr[:, t:t + 1], scale=frs[:, t:t + 1])
                last.then_inc(fx_ready, 1)

            def body(b, first, last=False):
                f = b - 1
                for k in range(STEPS):
                    if k == 3 and not first:
                        ffn_evacuate(f - 1, 1)
                    if k == 17:
                        ffn_evacuate(f, 0)
                    silu(f, k, first)
                    if k >= LAG_H:
                        upper(f, k - LAG_H, first)
                    elif not first:
                        upper(f - 1, STEPS + k - LAG_H, False)
                    if k == 6 and not first:
                        ffn_ln(f - 1, 1)
                    if k == 21:
                        ffn_ln(f, 0)
                    if last:
                        continue
                    if k == 4:
                        yT(b, 0)
                    if k == 5:
                        keys(b, 0)
                    if k == 7:
                        yT(b, 1)
                    if k == 8:
                        keys(b, 1)
                    if k == 10:
                        for u in range(NU):
                            exps(b, u)
                        factor(b)
                    if k == 13:
                        evacuate(b, 0)
                    if k == 15:
                        evacuate(b, 1)
                    if k == 17:
                        ln_attention(b, 0)
                    if k == 18:
                        ln_attention(b, 1)
                    if k == 23:
                        y2T(b, 0)
                    if k == 24:
                        y2T(b, 1)
                    if k == 26:
                        gate(b)

            act.wait_ge(prep_dve, 1)
            yT(0, 0)
            yT(0, 1)
            keys(0, 0)
            keys(0, 1)
            for u in range(NU):
                exps(0, u)
            factor(0)
            evacuate(0, 0)
            evacuate(0, 1)
            ln_attention(0, 0)
            ln_attention(0, 1)
            y2T(0, 0, alone=True)
            y2T(0, 1)
            gate(0)
            body(1, True)
            with act.Fori(2, NB) as b:
                body(b, False)
            body(NB, False, last=True)
            for k in range(STEPS - LAG_H, STEPS):
                upper(NB - 1, k, False)
            ffn_evacuate(NB - 1, 1)
            ffn_ln(NB - 1, 1)

        @block.vector
        def _(dve):
            v = nc.vector
            DVE_STEPS = 42
            PREP = 11
            n = [0, 0]

            def step(ins):
                n[1] += 1
                ins.then_inc(dve_step, 1)
                dve.wait_ge(dve_step, n[0] * DVE_STEPS + n[1] + PREP)

            def begin(b):
                n[0], n[1] = b, 0

            m = [0]

            def prep(ins):
                m[0] += 1
                ins.then_inc(dve_step, 1)
                dve.wait_ge(dve_step, m[0])

            def merge(st, mu, dif, vs, ve, step):
                v.tensor_tensor(mu, st[:, :, 1], st[:, :, 4], ALU.add)
                v.tensor_tensor(dif, st[:, :, 1], st[:, :, 4], ALU.subtract)
                step(v.tensor_tensor(vs, st[:, :, 2], st[:, :, 5], ALU.add))
                v.tensor_scalar(mu, mu, 0.5, None, ALU.mult)
                step(v.scalar_tensor_tensor(dif, dif, 0.25, dif, ALU.mult, ALU.mult))
                step(v.scalar_tensor_tensor(ve, vs, 1.0 / D, dif, ALU.mult, ALU.add))

            def x_statistics(b, h):
                for t in range(h * TPH, (h + 1) * TPH):
                    last = v.bn_stats(st[:, t, :], X[:, b, t, :])
                return last

            def x_merge(b, done):
                merge(st, mu[:, :], dif[:, :], vs[:, :], ve[:, :], step)
                v.tensor_scalar(ve[:, :], ve[:, :], EPS, None, ALU.add).then_inc(done, 1)

            def normalise(b, h):
                for i in range(h * TPH, (h + 1) * TPH):
                    last = v.tensor_scalar(Y[:, i, :], X[:, b, i, :], mu[:, i:i + 1], rs[:, i:i + 1],
                                           ALU.subtract, ALU.mult)
                return last

            def ln1_statistics(b, h, loaded=16 * NB):
                if h == 0:
                    dve.wait_ge(x_loaded, loaded)
                    x_statistics(b, 0)
                else:
                    step(x_statistics(b, 1))
                    x_merge(b, var1)

            def ln1(b, h):
                if h == 0:
                    dve.wait_ge(pow1, b + 1)
                normalise(b, h).then_inc(y_ready, 1)

            def yT(b, h):
                c = slice(h * HALF, (h + 1) * HALF)
                dve.wait_ge(yhi, NH * b + h + 1)
                v.tensor_tensor(YT_l[:, c], SC[h][:, :], YT_h[:, c].bitcast(F32), ALU.subtract).then_inc(ylo, 1)

            def keys(b, h):
                c = slice(h * HALF, (h + 1) * HALF)
                dve.wait_ge(khi, NH * b + h + 1)
                v.scalar_tensor_tensor(KK_l[:, c], SC[h][:, :], wqbk[:, :], KK_h[:, c].bitcast(F32),
                                       ALU.add, ALU.subtract).then_inc(klo, 1)

            def values(b, h):
                dve.wait_ge(v_ps, NH * b + h + 1)
                v.tensor_tensor(V[:, h * TPH:(h + 1) * TPH, :], SC[h][:, :].rearrange("p (t d) -> p t d", d=P),
                                bv_b[:, None, :].to_broadcast([P, TPH, P]), ALU.add).then_inc(v_ev, 1)

            def key_terms(b):
                dve.wait_ge(c_ps, b + 1)
                v.tensor_scalar(cs[:, :], SC[0][:, 0:2 * NT].rearrange("p (t two) -> p t two", two=2)[:, :, 0],
                                bqbk[:, :], SCALE, ALU.add, ALU.mult).then_inc(c_ev, 1)

            def shift(b, u):
                dve.wait_ge(sc_ps, NU * b + u + 1)
                step(v.tensor_reduce(nmax[:, u:u + 1], SC[u % 2][:, UNIT_COL[u]:HALF], AX.X, ALU.max, negate=True))
                v.tensor_scalar(nbias[:, u:u + 1], nmax[:, u:u + 1], SCALE, None, ALU.mult).then_inc(nb, 1)

            def maximum(b):
                dve.wait_ge(nb, NU * (b + 1))
                v.tensor_tensor(val[:, 0:TPH], cs[:, 0:TPH], nbias[:, 0:TPH], ALU.subtract)
                step(v.tensor_tensor(val[:, TPH:NU], cs[:, :], nbias[:, TPH:NU], ALU.subtract))
                v.tensor_reduce(mx[:, :], val[:, :], AX.X, ALU.max).then_inc(mx_ready, 1)
                dve.wait_ge(maxT_ps, b + 1)
                v.tensor_reduce(m1[:, :], SC[0][0:1, 0:P], AX.X, ALU.max).then_inc(m1_ready, 1)
                dve.wait_ge(maxB_ps, b + 1)
                v.tensor_scalar(nmg[:, :], SC[0][:, P:P + 1], -1.0, None, ALU.mult).then_inc(nmg_ready, 1)

            def sums(b):
                dve.wait_ge(fexp, b + 1)
                dve.wait_ge(exps_done, NU * (b + 1))
                step(v.tensor_tensor(rf[:, :], rsum[:, :], fac[:, :], ALU.mult))
                v.tensor_reduce(zp[:, :], rf[:, :], AX.X, ALU.add).then_inc(zp_ready, 1)

            def scale_values(b, h):
                u0, k = (0, TPH) if h == 0 else (TPH, NT)
                v.tensor_tensor(VP[:, u0:u0 + k, :], V[:, 0:k, :],
                                fac[:, u0:u0 + k, None].to_broadcast([P, k, P]), ALU.mult).then_inc(vp_ready, 1)

            def epsilon(b):
                dve.wait_ge(z_ps, b + 1)
                step(v.tensor_copy(zs[:, :], SC[0][:, P:P + 1]))
                v.tensor_scalar(ez[:, :], zs[:, :], zs[:, :], EPS, ALU.mult, ALU.mult).then_inc(ez_ready, 1)

            def o_statistics(b, h):
                dve.wait_ge(oT_ps, NH * b + h + 1)
                for t in range(TPH):
                    last = v.bn_stats(st[:, h * TPH + t, :], SC[1 - h][:, t * P:(t + 1) * P])
                if h == 1:
                    step(last)

            def o_merge(b):
                merge(st, mu[:, :], dif[:, :], vs[:, :], ve[:, :], step)
                dve.wait_ge(ez_ready, b + 1)
                v.tensor_scalar(ve[:, :], ve[:, :], ez[:, :], None, ALU.add).then_inc(var2, 1)

            def o_shift(b):
                dve.wait_ge(pow2, b + 1)
                v.scalar_tensor_tensor(nmr[:, :], mu[:, :], -1.0, rs[:, :], ALU.mult, ALU.mult).then_inc(nmr2, 1)

            def x1(b, h):
                dve.wait_ge(ox_ready, NH * b + h + 1)
                xh = X[:, b, h * TPH:(h + 1) * TPH, :]
                v.tensor_tensor(xh, xh, Y[:, h * TPH:(h + 1) * TPH, :], ALU.add).then_inc(x1_ready, 1)

            def ln2_statistics(b, h):
                if h == 1:
                    step(x_statistics(b, 1))
                    x_merge(b, var3)
                else:
                    x_statistics(b, 0)

            def ln2(b, h):
                if h == 0:
                    dve.wait_ge(pow3, b + 1)
                normalise(b, h).then_inc(y2_ready, 1)

            def y2T(b, h):
                c = slice(h * HALF, (h + 1) * HALF)
                dve.wait_ge(y2hi, NH * b + h + 1)
                hi, lo = [(Y2_h, Y2_l), (YT_h, YT_l)][h]
                v.tensor_tensor(lo[:, c], SC[h][:, :], hi[:, c].bitcast(F32), ALU.subtract).then_inc(y2lo, 1)

            full = [P, NT, NE]
            cube = [P, NT, NE, NE]

            def logits(b):
                dve.wait_ge(gate_ps, b + 1)
                lo_ = SC[0][:, 0:NT * NE].rearrange("p (t e) -> p t e", e=NE)
                step(v.tensor_reduce(gmax[:, :], lo_, AX.X, ALU.max))
                v.tensor_tensor(lg[:, :, :], lo_, gmax[:, :, None].to_broadcast(full), ALU.subtract
                                ).then_inc(lg_ready, 1)

            def rank_experts(b):
                dve.wait_ge(gexp, b + 1)
                step(v.tensor_reduce(gsum[:, :], eg[:, :, :], AX.X, ALU.add))
                step(v.reciprocal(grec[:, :], gsum[:, :]))
                step(v.tensor_tensor(pg[:, :, :], eg[:, :, :], grec[:, :, None].to_broadcast(full), ALU.mult))
                other = pg[:, :, None, :].to_broadcast(cube)
                own = pg[:, :, :, None].to_broadcast(cube)
                v.tensor_tensor(cmp_gt[:, :, :, :], other, own, ALU.is_gt)
                step(v.tensor_tensor(cmp_eq[:, :, :, :], other, own, ALU.is_equal))
                step(v.tensor_tensor(cmp_eq[:, :, :, :], cmp_eq[:, :, :, :],
                                     before[:, None, :, :].to_broadcast(cube), ALU.mult))

            def choose_experts(b):
                step(v.tensor_tensor(cmp_gt[:, :, :, :], cmp_gt[:, :, :, :], cmp_eq[:, :, :, :], ALU.add))
                step(v.tensor_reduce(rank[:, :, :], cmp_gt[:, :, :, :], AX.X, ALU.add))
                step(v.scalar_tensor_tensor(wsel[:, :, :], rank[:, :, :], 2.0, pg[:, :, :], ALU.is_lt, ALU.mult))
                step(v.tensor_reduce(gsum[:, :], wsel[:, :, :], AX.X, ALU.add))
                step(v.tensor_scalar(gsum[:, :], gsum[:, :], 1e-20, None, ALU.add))
                step(v.reciprocal(grec[:, :], gsum[:, :]))
                step(v.tensor_tensor(wn[:, :, :], wsel[:, :, :], grec[:, :, None].to_broadcast(full), ALU.mult))
                step(v.tensor_copy(whl[:, :, 0, :], wn[:, :, :]))
                v.tensor_tensor(whl[:, :, 1, :], wn[:, :, :], whl[:, :, 0, :].bitcast(F32), ALU.subtract
                                ).then_inc(whl_ready, 1)

            def weightsT(b, alone=False):
                if not alone:
                    dve.wait_ge(wb_ps, (b - 1) * ROUTED_STEPS + NR)
                dve.wait_ge(wT_ps, NH * b + 1)
                v.tensor_copy(wT[:, 0:HALF], SC[1][0:2 * NE, :]).then_inc(wT_ready, 1)
                dve.wait_ge(wT_ps, NH * (b + 1))
                step(v.tensor_copy(wT_next[:, :], SC[0][0:2 * NE, :]))
                assert n[1] == DVE_STEPS, n[1]

            def move_second_half(f, first):
                c = slice(HALF, T)
                if not first:
                    dve.wait_ge(u_ps, f * STEPS)
                v.tensor_copy(Y2_h[:, c], YT_h[:, c].bitcast(F32))
                v.tensor_copy(Y2_l[:, c], YT_l[:, c].bitcast(F32)).then_inc(y2_moved, 1)
                if not first:
                    dve.wait_ge(wb_ps, f * ROUTED_STEPS)
                v.tensor_copy(wT[:, c], wT_next[:, :].bitcast(F32)).then_inc(wT_moved, 1)

            def product(f, k, first):
                c, r = k % NC, rows(k % NC)
                dve.wait_ge(s_ready, f * STEPS + k + 1)
                dve.wait_ge(u_ps, f * STEPS + k + 1)
                if c < NR:
                    if c >= 2:
                        dve.wait_ge(h_ready, f * STEPS + k - 1)
                    v.tensor_tensor(TU[0:r, k % 2, :], S[0:r, k % 2, :], UB[k % 2][0:r, :], ALU.mult
                                    ).then_inc(u_used, 1)
                else:
                    if k >= RING or not first:
                        dve.wait_ge(lo_ready, f * STEPS + k + 1 - RING)
                    v.tensor_tensor(H[0:r, k % RING, :], S[0:r, k % 2, :], UB[k % 2][0:r, :], ALU.mult
                                    ).then_inc(h_ready, 1)

            def weigh(f, k, first):
                dve.wait_ge(u_used, f * ROUTED_STEPS + wb_count(k))
                dve.wait_ge(wb_ps, f * ROUTED_STEPS + wb_count(k))
                if k >= RING or not first:
                    dve.wait_ge(lo_ready, f * STEPS + k + 1 - RING)
                v.tensor_tensor(H[:, k % RING, :], TU[:, k % 2, :], WB[:, :], ALU.mult).then_inc(h_ready, 1)

            F_STEPS = 4 * NH

            def ffn_ln(f, g):
                count = [0]

                def fstep(ins):
                    count[0] += 1
                    ins.then_inc(f_step, 1)
                    dve.wait_ge(f_step, f * F_STEPS + g * 4 + count[0])

                dve.wait_ge(fT_ps, NH * f + g + 1)
                for t in range(TPH):
                    last = v.bn_stats(fst[:, t, :], SC[1][:, t * P:(t + 1) * P])
                fstep(last)
                merge(fst, fmu[:, :], fdif[:, :], fvs[:, :], fve[:, :], fstep)
                v.tensor_scalar(fve[:, :], fve[:, :], EPS, None, ALU.add).then_inc(var4, 1)

            def ffn_shift(f, g):
                dve.wait_ge(pow4, NH * f + g + 1)
                v.scalar_tensor_tensor(fnmr[:, :], fmu[:, :], -1.0, frs[:, :], ALU.mult, ALU.mult
                                       ).then_inc(nmr4, 1)

            def ffn_out(f, g):
                dve.wait_ge(fx_ready, NH * f + g + 1)
                xo = X[:, f, g * TPH:(g + 1) * TPH, :]
                v.tensor_tensor(xo, xo, FX[:, :, :], ALU.add).then_inc(out_ready, 1)

            def body(b, first, last=False):
                f = b - 1
                for k in range(STEPS):
                    if k % NC < NR:
                        product(f, k, first)
                        if k % NC:
                            weigh(f, k - LAG_W, first)
                    else:
                        if k % NC == NR:
                            weigh(f, k - LAG_W, first)
                        product(f, k, first)
                    if k == 0:
                        move_second_half(f, first)
                    if k == 4 and not first:
                        ffn_ln(f - 1, 1)
                    if k == 6 and not first:
                        ffn_shift(f - 1, 1)
                    if k == 7 and not first:
                        ffn_out(f - 1, 1)
                    if k == 19:
                        ffn_ln(f, 0)
                    if k == 21:
                        ffn_shift(f, 0)
                    if k == 22:
                        ffn_out(f, 0)
                    if last:
                        continue
                    if k == 0:
                        begin(b)
                        ln1_statistics(b, 0)
                    if k == 1:
                        ln1_statistics(b, 1)
                    if k == 2:
                        ln1(b, 0)
                    if k == 3:
                        ln1(b, 1)
                    if k == 4:
                        yT(b, 0)
                    if k == 5:
                        keys(b, 0)
                    if k == 7:
                        values(b, 0)
                        yT(b, 1)
                    if k == 8:
                        keys(b, 1)
                        key_terms(b)
                    if k == 9:
                        values(b, 1)
                    if k == 10:
                        for u in range(NU):
                            shift(b, u)
                        maximum(b)
                        sums(b)
                        scale_values(b, 0)
                    if k == 11:
                        scale_values(b, 1)
                    if k == 12:
                        epsilon(b)
                    if k == 15:
                        o_statistics(b, 0)
                    if k == 16:
                        o_statistics(b, 1)
                        o_merge(b)
                    if k == 17:
                        o_shift(b)
                    if k == 18:
                        x1(b, 0)
                        x1(b, 1)
                        dve.wait_ge(x1_ready, NH * (b + 1))
                    if k == 19:
                        ln2_statistics(b, 0)
                    if k == 20:
                        ln2_statistics(b, 1)
                    if k == 21:
                        ln2(b, 0)
                    if k == 22:
                        ln2(b, 1)
                    if k == 23:
                        y2T(b, 0)
                    if k == 24:
                        y2T(b, 1)
                    if k == 25:
                        logits(b)
                    if k == 26:
                        rank_experts(b)
                    if k == 27:
                        choose_experts(b)
                if not last:
                    weightsT(b)

            prep(v.memset(wkbq_s[:, :], 0.0))
            dve.wait_ge(small_loaded, 16 * 7)
            prep(v.tensor_copy(Wv_h[:, :], Wv_s[:, :]))
            prep(v.tensor_tensor(Wv_l[:, :], Wv_s[:, :], Wv_h[:, :].bitcast(F32), ALU.subtract))
            dve.wait_ge(prep_act, 1)
            prep(v.tensor_copy(gwT_h[:, :], gwT_s[:, :]))
            prep(v.tensor_tensor(gwT_l[:, :], gwT_s[:, :], gwT_h[:, :].bitcast(F32), ALU.subtract))
            dve.wait_ge(prep_ps, 2)
            prep(v.tensor_copy(A_h[:, :], SC[1][:, 0:P]))
            prep(v.tensor_tensor(A_l[:, :], SC[1][:, 0:P], A_h[:, :].bitcast(F32), ALU.subtract))
            prep(v.tensor_copy(wqbk[:, :], SC[1][:, P:P + 1]))
            prep(v.tensor_copy(wkbq_s[:, 0:1], SC[1][:, P + 1:P + 2]))
            prep(v.tensor_copy(bqbk[:, :], SC[1][:, P + 2:P + 3]))
            prep(v.tensor_copy(wkbq_h[:, :], wkbq_s[:, :]))
            v.tensor_tensor(wkbq_l[:, :], wkbq_s[:, :], wkbq_h[:, :].bitcast(F32), ALU.subtract
                            ).then_inc(prep_dve, 1)
            begin(0)
            ln1_statistics(0, 0, loaded=16)
            ln1_statistics(0, 1)
            ln1(0, 0)
            ln1(0, 1)
            yT(0, 0)
            yT(0, 1)
            keys(0, 0)
            keys(0, 1)
            values(0, 0)
            values(0, 1)
            key_terms(0)
            for u in range(NU):
                shift(0, u)
            maximum(0)
            sums(0)
            scale_values(0, 0)
            scale_values(0, 1)
            epsilon(0)
            o_statistics(0, 0)
            o_statistics(0, 1)
            o_merge(0)
            o_shift(0)
            x1(0, 0)
            x1(0, 1)
            dve.wait_ge(x1_ready, NH)
            ln2_statistics(0, 0)
            ln2_statistics(0, 1)
            ln2(0, 0)
            ln2(0, 1)
            y2T(0, 0)
            y2T(0, 1)
            logits(0)
            rank_experts(0)
            choose_experts(0)
            weightsT(0, alone=True)
            body(1, True)
            with dve.Fori(2, NB) as b:
                body(b, False)
            body(NB, False, last=True)
            ffn_ln(NB - 1, 1)
            ffn_shift(NB - 1, 1)
            ffn_out(NB - 1, 1)


_INS = ["L0_attn_x", "L0_attn_Wq", "L0_attn_bq", "L0_attn_Wk", "L0_attn_bk", "L0_attn_Wv", "L0_attn_bv",
        "L0_ffn_gate_w", "L0_ffn_wg", "L0_ffn_wu", "L0_ffn_wd", "L0_ffn_swg", "L0_ffn_swu", "L0_ffn_swd"]


def kernel(**inputs):
    import concourse.bacc as _bacc
    from concourse.bass_utils import run_bass_kernel_spmd as _run

    nc = _bacc.Bacc("TRN2", target_bir_lowering=False, num_devices=1)
    arrays, args = {}, []
    for name in _INS:
        a = np.ascontiguousarray(inputs[name])
        arrays[f"in_{name}"] = a
        args.append(nc.dram_tensor(f"in_{name}", a.shape, mybir.dt.from_np(a.dtype), kind="ExternalInput").ap())
    args.append(nc.dram_tensor("out_0", (NB, T, D), F32, kind="ExternalOutput").ap())
    sandwich(nc, *args)
    r = _run(nc, [arrays], core_ids=[0])
    return r.results[0]["out_0"]
```

```python
from contextlib import ExitStack

import numpy as np

import concourse.bass as bass
from concourse import mybir

P = 128
NB, T, D = 4, 1024, 128
NT = T // P
HALF = 512
NH = T // HALF
TPH = HALF // P
NE, I, NS = 8, 176, 2
ROUTED, SHARED = NE * I, NS * I
FF = ROUTED + SHARED
NR = ROUTED // P
NC = -(-FF // P)
LASTC = FF - (NC - 1) * P
STEPS = NH * NC
ROUTED_STEPS = NH * NR
LAG_W, LAG_H, LAG_D = 1, 2, 4
SCORES_AT = 6
RING = 4
EPS = 1e-5
SCALE = float(D) ** -0.5
NEG = -1e30

UNITS = [(h, j) for h in range(NH) for j in range(TPH * (h + 1))]
NU = len(UNITS)
UNIT_COL = [max(0, P * j - HALF * h) for h, j in UNITS]
UNIT_AT = [sum(HALF - c for c in UNIT_COL[:u]) for u in range(NU)]
E_COLS = sum(HALF - c for c in UNIT_COL)

F32 = mybir.dt.float32
F32R = mybir.dt.float32r
BF16 = mybir.dt.bfloat16
ALU = mybir.AluOpType
ACT = mybir.ActivationFunctionType
AX = mybir.AxisListType


def rows(c):
    return LASTC if c == NC - 1 else P


def wb_count(k):
    return (k // NC) * NR + min(k % NC + 1, NR)


def routed_step(i):
    return (i // NR) * NC + i % NR


def sandwich(nc, x, Wq, bq, Wk, bk, Wv, bv, gate_w, wg, wu, wd, swg, swu, swd, out):
    ctx = ExitStack()
    with ctx:
        def sb(name, shape, dt=F32):
            return ctx.enter_context(nc.sbuf_tensor(name, shape, dt))

        def sem(name):
            return ctx.enter_context(nc.semaphore(name))

        ident = sb("ident", [P, P])
        identb = sb("identb", [P, P], BF16)
        ones = sb("ones", [P, P])
        maskb = sb("maskb", [P, P], BF16)
        before = sb("before", [P, NE, NE])
        neg_half = sb("neg_half", [P, NT])
        sel_two = sb("sel_two", [2 * NE, 2, ROUTED], BF16)
        sel = sb("sel", [2 * NE, ROUTED], F32R)
        Wqk_s = sb("Wqk_s", [P, 2, P])
        WqkT = sb("WqkT", [P, 2, P])
        Wv_s = sb("Wv_s", [P, P])
        bqk = sb("bqk", [P, 2])
        bq_rep = sb("bq_rep", [P, P])
        bv_b = sb("bv_b", [P, P])
        gw_s = sb("gw_s", [NE, P])
        A_h, A_l = sb("A_h", [P, P], F32R), sb("A_l", [P, P], F32R)
        wkbq_rep = sb("wkbq_rep", [P, P])
        wqbk = sb("wqbk", [P, 1])
        bqbk = sb("bqbk", [P, 1])
        gwT_s = sb("gwT_s", [P, NE])
        Wd_s = sb("Wd_s", [P, NC, P])
        Wg_h, Wg_l = sb("Wg_h", [P, FF], F32R), sb("Wg_l", [P, FF], F32R)
        Wu_h, Wu_l = sb("Wu_h", [P, FF], F32R), sb("Wu_l", [P, FF], F32R)
        Wd_h, Wd_l = sb("Wd_h", [P, NC, P], F32R), sb("Wd_l", [P, NC, P], F32R)

        X = sb("X", [P, NB, NT, P])
        Y = sb("Y", [P, NT, P])
        YT_h, YT_l = sb("YT_h", [P, T], F32R), sb("YT_l", [P, T], F32R)
        YF = sb("YF", [P, T])
        KK_h, KK_l = sb("KK_h", [P, T], F32R), sb("KK_l", [P, T], F32R)
        V = sb("V", [P, NT, P])
        VP = sb("VP", [P, NU, P])
        E = sb("E", [P, E_COLS])
        OT = sb("OT", [P, T])
        Y2_h, Y2_l = sb("Y2_h", [P, T], F32R), sb("Y2_l", [P, T], F32R)
        st = sb("st", [P, NT, 6])
        mu, dif, vs = sb("mu", [P, NT]), sb("dif", [P, NT]), sb("vs", [P, NT])
        ve = sb("ve", [P, NT])
        rs = sb("rs", [P, NT])
        st_x = sb("st_x", [P, NT, 6])
        mu_x, dif_x, vs_x = sb("mu_x", [P, NT]), sb("dif_x", [P, NT]), sb("vs_x", [P, NT])
        ve_x = sb("ve_x", [P, NT])
        rs_x = sb("rs_x", [P, NT])
        nbias = sb("nbias", [P, NU])
        rsum = sb("rsum", [P, NU])
        cs = sb("cs", [P, NT])
        val = sb("val", [P, NU])
        mx = sb("mx", [P, 1])
        m1 = sb("m1", [1, 1])
        nmg = sb("nmg", [P, 1])
        fac = sb("fac", [P, NU])
        rf = sb("rf", [P, NU])
        zp = sb("zp", [P, 1])
        zs = sb("zs", [P, 1])
        ez = sb("ez", [P, 1])
        scratch = sb("scratch", [P, 1])
        gmax = sb("gmax", [P, NT])
        lg = sb("lg", [P, NT, NE])
        eg = sb("eg", [P, NT, NE])
        gsum = sb("gsum", [P, NT])
        grec = sb("grec", [P, NT])
        pg = sb("pg", [P, NT, NE])
        cmp_gt = sb("cmp_gt", [P, NT, NE, NE])
        cmp_eq = sb("cmp_eq", [P, NT, NE, NE])
        rank = sb("rank", [P, NT, NE])
        wsel = sb("wsel", [P, NT, NE])
        wn = sb("wn", [P, NT, NE])
        whl = sb("whl", [P, NT, 2, NE], F32R)
        wT = sb("wT", [2 * NE, T], F32R)
        work = sb("work", [P, (2 + 2 + RING) * HALF])
        ring = work[:, :].rearrange("p (n t) -> p n t", t=HALF)
        S = ring[:, 0:2, :]
        TU = ring[:, 2:4, :]
        H = ring[:, 4:4 + RING, :]
        WS = sb("WS", [P, 2, HALF])
        Wg_s, Wu_s = work[:, 0:FF], work[:, FF:2 * FF]
        H_h, H_l = sb("H_h", [P, RING, HALF], F32R), sb("H_l", [P, RING, HALF], F32R)
        OF = sb("OF", [P, NH, HALF])
        fst = sb("fst", [P, TPH, 6])
        fmu, fdif, fvs = sb("fmu", [P, TPH]), sb("fdif", [P, TPH]), sb("fvs", [P, TPH])
        fve = sb("fve", [P, TPH])
        frs = sb("frs", [P, TPH])
        FX = sb("FX", [P, TPH, P])

        def bank(name):
            return ctx.enter_context(nc.psum_tensor(name, [P, HALF], F32))

        SC = [bank("SC0"), bank("SC1")]
        GB, UB = [bank("GB0"), bank("GB1")], [bank("UB0"), bank("UB1")]
        WB, DB = bank("WB"), bank("DB")

        def score_banks(b):
            return 6 if isinstance(b, int) and b == 0 else 2

        def score_bank(b, u):
            return (SC + GB + UB)[u % score_banks(b)]

        x_first_half = sem("x_first_half")
        x_loaded = sem("x_loaded")
        small_loaded = sem("small_loaded")
        values_loaded = sem("values_loaded")
        wg_loaded = sem("wg_loaded")
        wu_loaded = sem("wu_loaded")
        wd_loaded = sem("wd_loaded")
        out_stored = sem("out_stored")
        ident_ready = sem("ident_ready")
        identb_ready = sem("identb_ready")
        consts = sem("consts")
        pool_step = sem("pool_step")
        prep_ps = sem("prep_ps")
        prep_act = sem("prep_act")
        prep_dve = sem("prep_dve")
        wgu_split = sem("wgu_split")
        wu_upper = sem("wu_upper")
        wd_upper = sem("wd_upper")
        wd_split = sem("wd_split")
        var1 = sem("var1")
        pow1 = sem("pow1")
        y_ready = sem("y_ready")
        yT_ps = sem("yT_ps")
        yhi = sem("yhi")
        ylo = sem("ylo")
        kk_ps = sem("kk_ps")
        khi = sem("khi")
        klo = sem("klo")
        v_ps = sem("v_ps")
        v_ev = sem("v_ev")
        c_ev = sem("c_ev")
        sc_ps = sem("sc_ps")
        nb = sem("nb")
        exps_done = sem("exps_done")
        mx_ready = sem("mx_ready")
        maxT_ps = sem("maxT_ps")
        m1_ready = sem("m1_ready")
        maxB_ps = sem("maxB_ps")
        nmg_ready = sem("nmg_ready")
        fexp = sem("fexp")
        zp_ready = sem("zp_ready")
        z_ps = sem("z_ps")
        vp_ready = sem("vp_ready")
        ez_ready = sem("ez_ready")
        pv_ps = sem("pv_ps")
        o_ev = sem("o_ev")
        oT_ps = sem("oT_ps")
        var2 = sem("var2")
        pow2 = sem("pow2")
        x1_ready = sem("x1_ready")
        var3 = sem("var3")
        pow3 = sem("pow3")
        y2_ready = sem("y2_ready")
        y2T_ps = sem("y2T_ps")
        y2whole = sem("y2whole")
        y2hi = sem("y2hi")
        y2lo = sem("y2lo")
        gate_ps = sem("gate_ps")
        lg_ready = sem("lg_ready")
        gexp = sem("gexp")
        whl_ready = sem("whl_ready")
        wT_ps = sem("wT_ps")
        wT_ready = sem("wT_ready")
        y2_moved = sem("y2_moved")
        gate_step = sem("gate_step")
        ties_ready = sem("ties_ready")
        prep_step = sem("prep_step")
        g_ps = sem("g_ps")
        u_ps = sem("u_ps")
        wb_ps = sem("wb_ps")
        ws_ready = sem("ws_ready")
        d_ps = sem("d_ps")
        s_ready = sem("s_ready")
        u_used = sem("u_used")
        h_ready = sem("h_ready")
        hi_ready = sem("hi_ready")
        lo_ready = sem("lo_ready")
        fo_ev = sem("fo_ev")
        f_step = sem("f_step")
        fT_ps = sem("fT_ps")
        var4 = sem("var4")
        pow4 = sem("pow4")
        f_centred = sem("f_centred")
        c_products = sem("c_products")
        o_centred = sem("o_centred")
        out_ready = sem("out_ready")
        dve_step = sem("dve_step")

        def split3(out_ap, wh, wl, xh, xl):
            nc.tensor.matmul(out_ap, wh, xh, start=True, stop=False)
            nc.tensor.matmul(out_ap, wh, xl, start=False, stop=False)
            return nc.tensor.matmul(out_ap, wl, xh, start=False, stop=True)

        block = ctx.enter_context(nc.Block())

        @block.sync
        def _(sp):
            xt = x.rearrange("b (t p) d -> b p t d", p=P)
            ot = out.rearrange("b (g t p) d -> b g p t d", g=NH, p=P)
            sp.dma_start(X[:, 0, 0:TPH, :], xt[0][:, 0:TPH, :]).then_inc(x_first_half, 16)
            sp.dma_start(Wqk_s[:, 0, :], Wq).then_inc(small_loaded, 16)
            sp.dma_start(Wqk_s[:, 1, :], Wk).then_inc(small_loaded, 16)
            sp.dma_start(X[:, 0, TPH:NT, :], xt[0][:, TPH:NT, :]).then_inc(x_loaded, 16)
            sp.dma_start(bqk[:, 0:1], bq.rearrange("(p o) -> p o", o=1)).then_inc(small_loaded, 16)
            sp.dma_start(bqk[:, 1:2], bk.rearrange("(p o) -> p o", o=1)).then_inc(small_loaded, 16)
            sp.dma_start(gw_s[:, :], gate_w).then_inc(small_loaded, 16)
            sp.dma_start(Wv_s[:, :], Wv).then_inc(values_loaded, 16)
            sp.dma_start(bv_b[:, :], bv.rearrange("(o d) -> o d", o=1).to_broadcast([P, P])
                         ).then_inc(values_loaded, 16)
            rt = slice(0, ROUTED)
            sh = slice(ROUTED, FF)
            sp.dma_start(Wg_s[:, rt].rearrange("p (e i) -> p e i", e=NE),
                         wg.rearrange("e h i -> h e i")).then_inc(wg_loaded, 16)
            sp.dma_start(Wg_s[:, sh], swg).then_inc(wg_loaded, 16)
            sp.dma_start(Wu_s[:, rt].rearrange("p (e i) -> p e i", e=NE),
                         wu.rearrange("e h i -> h e i")).then_inc(wu_loaded, 16)
            sp.dma_start(Wu_s[:, sh], swu).then_inc(wu_loaded, 16)
            sp.dma_start(Wd_s[:, 0:NR, :], wd.rearrange("e i h -> (e i) h").rearrange("(c p) h -> p c h", p=P)
                         ).then_inc(wd_loaded, 16)
            full = NC - 1 - NR
            sp.dma_start(Wd_s[:, NR:NC - 1, :], swd[0:full * P, :].rearrange("(c p) h -> p c h", p=P)
                         ).then_inc(wd_loaded, 16)
            sp.dma_start(Wd_s[0:LASTC, NC - 1, :], swd[full * P:SHARED, :]).then_inc(wd_loaded, 16)
            for b in range(1, NB):
                sp.wait_ge(x_loaded, 16 * b)
                sp.dma_start(X[:, b, :, :], xt[b]).then_inc(x_loaded, 16)
            for b in range(NB):
                for g in range(NH):
                    sp.wait_ge(out_ready, NH * b + g + 1)
                    sp.dma_start(ot[b, g], X[:, b, g * TPH:(g + 1) * TPH, :]).then_inc(out_stored, 16)
            sp.wait_ge(out_stored, 16 * NB * NH)

        @block.gpsimd
        def _(pool):
            n = [0]

            def step(ins):
                n[0] += 1
                ins.then_inc(pool_step, 1)
                pool.wait_ge(pool_step, n[0])

            step(nc.gpsimd.memset(ident[:, :], 0.0))
            step(nc.gpsimd.affine_select(out=ident[:, :], in_=ident[:, :], compare_op=ALU.not_equal, fill=1.0,
                                         base=0, pattern=[[-1, P]], channel_multiplier=1))
            nc.gpsimd.memset(neg_half[:, :], -0.5).then_inc(ident_ready, 1)
            nc.gpsimd.memset(ones[:, :], 1.0)
            step(nc.gpsimd.memset(maskb[:, :], 0.0))
            nc.gpsimd.affine_select(out=maskb[:, :], in_=maskb[:, :], compare_op=ALU.is_ge, fill=NEG,
                                    base=0, pattern=[[1, P]], channel_multiplier=-1).then_inc(consts, 1)

            step(nc.gpsimd.memset(before[:, :, :], 1.0))
            step(nc.gpsimd.affine_select(out=before[:, :, :], in_=before[:, :, :], compare_op=ALU.is_ge, fill=0.0,
                                         base=-1, pattern=[[1, NE], [-1, NE]], channel_multiplier=0))
            step(nc.gpsimd.memset(sel_two[:, :, :], 1.0))

            def power(dst, src, width):
                return nc.gpsimd.tensor_tensor(dst, src, neg_half[:, 0:width], ALU.pow)

            def pow_ln1(b, h):
                half = slice(h * TPH, (h + 1) * TPH)
                pool.wait_ge(var1, NH * b + h + 1)
                power(rs_x[:, half], ve_x[:, half], TPH).then_inc(pow1, 1)

            def pow_attention(b, h):
                half = slice(h * TPH, (h + 1) * TPH)
                pool.wait_ge(var2, NH * b + h + 1)
                power(rs[:, half], ve[:, half], TPH).then_inc(pow2, 1)

            def pow_ln2(b, h):
                half = slice(h * TPH, (h + 1) * TPH)
                pool.wait_ge(var3, NH * b + h + 1)
                power(rs[:, half], ve[:, half], TPH).then_inc(pow3, 1)

            def key_products(b, h):
                half = slice(h * TPH, (h + 1) * TPH)
                pool.wait_ge(y_ready, NH * b + h + 1)
                nc.gpsimd.tensor_tensor(OT[:, :].rearrange("p (t d) -> p t d", d=P)[:, half, :], Y[:, half, :],
                                        wkbq_rep[:, None, :].to_broadcast([P, TPH, P]), ALU.mult
                                        ).then_inc(c_products, 1)

            pow_ln1(0, 0)
            pow_ln1(0, 1)
            pool.wait_ge(prep_dve, 1)
            key_products(0, 0)
            key_products(0, 1)
            step(nc.gpsimd.affine_select(out=sel_two[:, :, :], in_=sel_two[:, :, :], compare_op=ALU.is_ge, fill=0.0,
                                         base=0, pattern=[[ROUTED, 2], [1, ROUTED]], channel_multiplier=-I))
            step(nc.gpsimd.affine_select(out=sel_two[:, :, :], in_=sel_two[:, :, :], compare_op=ALU.is_ge, fill=0.0,
                                         base=I - 1, pattern=[[-ROUTED, 2], [-1, ROUTED]], channel_multiplier=I))
            nc.gpsimd.tensor_tensor(sel[:, :], sel_two[:, 0, :], sel_two[:, 1, :], ALU.add
                                    ).then_inc(consts, 1)

            def split(hi, lo, src):
                step(nc.gpsimd.tensor_copy(hi, src))
                return nc.gpsimd.tensor_tensor(lo, src, hi.bitcast(F32), ALU.subtract)

            pool.wait_ge(wg_loaded, 32)
            split(Wg_h[:, :], Wg_l[:, :], Wg_s[:, :]).then_inc(wgu_split, 1)
            pool.wait_ge(wu_upper, 1)
            nc.gpsimd.tensor_tensor(Wu_l[:, :], Wu_s[:, :], Wu_h[:, :].bitcast(F32), ALU.subtract
                                    ).then_inc(wgu_split, 1)
            pow_ln1(1, 0)
            pow_ln1(1, 1)
            pow_attention(0, 0)
            pow_ln2(0, 0)
            pow_attention(0, 1)
            pow_ln2(0, 1)
            key_products(1, 0)
            key_products(1, 1)
            pool.wait_ge(wd_upper, 1)
            nc.gpsimd.tensor_tensor(Wd_l[:, 0:NC - 1, :], Wd_s[:, 0:NC - 1, :], Wd_h[:, 0:NC - 1, :].bitcast(F32),
                                    ALU.subtract)
            nc.gpsimd.tensor_tensor(Wd_l[0:LASTC, NC - 1, :], Wd_s[0:LASTC, NC - 1, :],
                                    Wd_h[0:LASTC, NC - 1, :].bitcast(F32), ALU.subtract).then_inc(wd_split, 1)

            def lower(f, k, first):
                r = rows(k % NC)
                pool.wait_ge(h_ready, f * STEPS + k + 1)
                pool.wait_ge(hi_ready, f * STEPS + k + 1)
                if k >= RING or not first:
                    pool.wait_ge(d_ps, f * STEPS + k + 1 - RING)
                q = k % RING
                nc.gpsimd.tensor_tensor(H_l[0:r, q, :], H[0:r, q, :], H_h[0:r, q, :].bitcast(F32),
                                        ALU.subtract).then_inc(lo_ready, 1)

            def ffn_pow(f, g):
                pool.wait_ge(var4, NH * f + g + 1)
                power(frs[:, :], fve[:, :], TPH).then_inc(pow4, 1)

            def body(b, first, last=False):
                f = b - 1
                for k in range(STEPS):
                    if k >= LAG_H:
                        lower(f, k - LAG_H, first)
                    elif not first:
                        lower(f - 1, STEPS + k - LAG_H, False)
                    if k == (7 if last else 18) and not first:
                        ffn_pow(f - 1, 1)
                    if k == (19 if last else 25):
                        ffn_pow(f, 0)
                    if last:
                        continue
                    if k == 8:
                        pow_attention(b, 0)
                        pow_ln2(b, 0)
                    if k == 10:
                        pow_attention(b, 1)
                    if k == 12:
                        pow_ln2(b, 1)
                    if k == 13:
                        pow_ln1(b + 1, 0)
                    if k == 18:
                        pow_ln1(b + 1, 1)
                    if k == 20:
                        key_products(b + 1, 0)
                    if k == 21:
                        key_products(b + 1, 1)

            body(1, True)
            with pool.Fori(2, NB) as b:
                body(b, False)
            body(NB, False, last=True)
            for k in range(STEPS - LAG_H, STEPS):
                lower(NB - 1, k, False)
            ffn_pow(NB - 1, 1)

        @block.tensor
        def _(pe):
            pe.wait_ge(consts, 1)
            pe.wait_ge(small_loaded, 16 * 5)
            nc.tensor.transpose(SC[0][:, 0:P], Wqk_s[:, 0, :], ident[:, :])
            nc.tensor.transpose(SC[0][:, P:2 * P], Wqk_s[:, 1, :], ident[:, :])
            nc.tensor.transpose(SC[0][:, 2 * P:2 * P + NE], gw_s[:, :], ident[0:NE, 0:NE]
                                ).then_inc(prep_ps, 1)
            pe.wait_ge(prep_act, 1)
            nc.tensor.matmul(GB[0][:, 0:P], WqkT[:, 1, :], WqkT[:, 0, :], start=True, stop=True)
            nc.tensor.matmul(GB[0][:, P:P + 1], WqkT[:, 0, :], bqk[:, 1:2], start=True, stop=True)
            nc.tensor.matmul(GB[0][:, P + 1:P + 2], bq_rep[:, :], bqk[:, 1:2], start=True, stop=True)
            nc.tensor.matmul(GB[0][:, 2 * P:3 * P], bq_rep[:, :], WqkT[:, 1, :], start=True, stop=True
                             ).then_inc(prep_ps, 1)

            def transposes(dst, src):
                for t in range(TPH):
                    last = nc.tensor.transpose(dst[:, t * P:(t + 1) * P], src(t), ident[:, :])
                return last

            def yT(b, h, alone=False):
                if h == 0 and not alone:
                    pe.wait_ge(lg_ready, b)
                if h == 1 and not alone:
                    pe.wait_ge(wT_ready, NH * (b - 1) + 1)
                pe.wait_ge(y_ready, NH * b + h + 1)
                transposes(SC[h], lambda t: Y[:, h * TPH + t, :]).then_inc(yT_ps, 1)

            def keys(b, h):
                c = slice(h * HALF, (h + 1) * HALF)
                pe.wait_ge(ylo, NH * b + h + 1)
                split3(SC[h][:, :], A_h[:, :], A_l[:, :], YT_h[:, c], YT_l[:, c]).then_inc(kk_ps, 1)

            def values(b, h, alone=False):
                bank = [WB, DB][h] if alone else SC[h]
                pe.wait_ge(klo, NH * b + h + 1)
                for t in range(TPH):
                    i = h * TPH + t
                    last = nc.tensor.matmul(bank[:, t * P:(t + 1) * P], YF[:, i * P:(i + 1) * P], Wv_s[:, :],
                                            start=True, stop=True)
                last.then_inc(v_ps, 1)

            def scores(b, u, alone=False):
                h, j = UNITS[u]
                c0 = UNIT_COL[u]
                if u < 2 and alone:
                    pe.wait_ge(klo, u + 1)
                elif u == 0:
                    pe.wait_ge(wT_ready, NH * b)
                elif u == 1:
                    pe.wait_ge(v_ev, NH * (b + 1))
                elif u >= score_banks(b):
                    pe.wait_ge(exps_done, NU * b + u + 1 - score_banks(b))
                bank = score_bank(b, u)
                dst = bank[:, c0:HALF]
                q = slice(h * HALF + c0, (h + 1) * HALF)
                kt = slice(j * P, (j + 1) * P)
                diag = j * P >= h * HALF
                nc.tensor.matmul(dst, KK_h[:, kt], YT_h[:, q], start=True, stop=False)
                nc.tensor.matmul(dst, KK_h[:, kt], YT_l[:, q], start=False, stop=False)
                last = nc.tensor.matmul(dst, KK_l[:, kt], YT_h[:, q], start=False, stop=not diag)
                if diag:
                    last = nc.tensor.matmul(bank[:, c0:c0 + P], identb[:, :], maskb[:, :],
                                            start=False, stop=True)
                last.then_inc(sc_ps, 1)

            def max_row(b):
                pe.wait_ge(exps_done, NU * (b + 1))
                pe.wait_ge(mx_ready, b + 1)
                nc.tensor.transpose(SC[0][0:1, 0:P], mx[:, :], ident[:, :]).then_inc(maxT_ps, 1)

            def max_all(b):
                pe.wait_ge(m1_ready, b + 1)
                nc.tensor.matmul(SC[0][:, P:P + 1], ones[0:1, :], m1[:, :], start=True, stop=True
                                 ).then_inc(maxB_ps, 1)

            def sum_all(b):
                pe.wait_ge(zp_ready, b + 1)
                nc.tensor.matmul(SC[0][:, P:P + 1], ones[:, :], zp[:, :], start=True, stop=True
                                 ).then_inc(z_ps, 1)

            def attend(b, h, j0, j1):
                pe.wait_ge(vp_ready, NH * b + h + 1)
                if h == 1:
                    pe.wait_ge(ez_ready, b + 1)
                end = TPH * (h + 1)
                for j in range(j0, j1):
                    u = UNITS.index((h, j))
                    c0 = UNIT_COL[u]
                    last = nc.tensor.matmul(SC[1 - h][:, c0:HALF], VP[:, u, :],
                                            E[:, UNIT_AT[u]:UNIT_AT[u] + HALF - c0], start=j == 0, stop=j == end - 1)
                if j1 == end:
                    last.then_inc(pv_ps, 1)

            def oT(b, h):
                pe.wait_ge(o_ev, NH * b + h + 1)
                transposes(SC[1 - h], lambda t: OT[:, (h * TPH + t) * P:(h * TPH + t + 1) * P]).then_inc(oT_ps, 1)

            def y2T(b, h):
                if h == 0:
                    pe.wait_ge(o_centred, NH * (b + 1))
                pe.wait_ge(y2_ready, NH * b + h + 1)
                transposes(SC[h], lambda t: Y[:, h * TPH + t, :]).then_inc(y2T_ps, 1)

            def gate(b, alone=False):
                if not alone:
                    pe.wait_ge(f_centred, NH * (b - 1))
                pe.wait_ge(y2lo, NH * b + 1)
                pe.wait_ge(y2whole, NH * (b + 1))
                for t in range(NT):
                    last = nc.tensor.matmul(SC[0][:, NE * t:NE * (t + 1)], YF[:, t * P:(t + 1) * P], gwT_s[:, :],
                                            start=True, stop=True)
                last.then_inc(gate_ps, 1)

            def weightsT(b, h, alone=False, last=False):
                if h == 0 and not alone:
                    pe.wait_ge(f_centred, NH * (b - 1) + 1)
                if h == 1 and not last:
                    pe.wait_ge(v_ev, NH * (b + 1) + 1)
                if h == 1 and last:
                    pe.wait_ge(klo, NH * (b + 1) + 1)
                pe.wait_ge(whl_ready, NH * b + h + 1)
                for t in range(TPH):
                    last = nc.tensor.transpose(SC[1 - h][0:2 * NE, t * P:(t + 1) * P],
                                               whl[:, h * TPH + t, :, :].rearrange("p a e -> p (a e)").bitcast(F32),
                                               ident[:, :])
                last.then_inc(wT_ps, 1)

            def projections(f, k, first):
                g, c = divmod(k, NC)
                r = rows(c)
                ic = slice(c * P, c * P + r)
                tok = slice(g * HALF, (g + 1) * HALF)
                if k == 0:
                    pe.wait_ge(y2lo, NH * f + 1)
                if k == NC:
                    pe.wait_ge(y2_moved, f + 1)
                if k >= 2 or not first:
                    pe.wait_ge(s_ready, f * STEPS + k - 1)
                split3(GB[k % 2][0:r, :], Wg_h[:, ic], Wg_l[:, ic], Y2_h[:, tok], Y2_l[:, tok]).then_inc(g_ps, 1)
                if k >= 2 and (k - 2) % NC < NR:
                    pe.wait_ge(u_used, f * ROUTED_STEPS + wb_count(k - 2))
                elif k >= 2 or not first:
                    pe.wait_ge(h_ready, f * STEPS + k - 1)
                split3(UB[k % 2][0:r, :], Wu_h[:, ic], Wu_l[:, ic], Y2_h[:, tok], Y2_l[:, tok]).then_inc(u_ps, 1)

            def weights(f, k, first):
                g, c = divmod(k, NC)
                if c >= NR:
                    return
                if c == 0:
                    pe.wait_ge(wT_ready, NH * f + g + 1)
                if k > 0 or not first:
                    pe.wait_ge(ws_ready, f * ROUTED_STEPS + wb_count(k) - 1)
                nc.tensor.matmul(WB[:, :], sel[:, c * P:(c + 1) * P], wT[:, g * HALF:(g + 1) * HALF],
                                 start=True, stop=True).then_inc(wb_ps, 1)

            def down(f, k, first):
                c, r = k % NC, rows(k % NC)
                if c == 0 and (k > 0 or not first):
                    pe.wait_ge(fo_ev, NH * f + k // NC)
                if k == 0 and first:
                    pe.wait_ge(wd_split, 1)
                pe.wait_ge(hi_ready, f * STEPS + k + 1)
                q = k % RING
                nc.tensor.matmul(DB[:, :], Wd_h[0:r, c, :], H_h[0:r, q, :], start=c == 0, stop=False)
                nc.tensor.matmul(DB[:, :], Wd_l[0:r, c, :], H_h[0:r, q, :], start=False, stop=False)
                pe.wait_ge(lo_ready, f * STEPS + k + 1)
                last = nc.tensor.matmul(DB[:, :], Wd_h[0:r, c, :], H_l[0:r, q, :], start=False, stop=c == NC - 1)
                last.then_inc(d_ps, 1)

            def fT(f, g, b=None):
                bank = SC[1 - g]
                if b is not None and g == 1:
                    pe.wait_ge(y2lo, NH * b + 1)
                if b is not None and g == 0:
                    pe.wait_ge(y2lo, NH * (b + 1))
                if b is None and g == 1:
                    pe.wait_ge(wT_ready, NH * (f + 1 if f == NB - 1 else f + 2))
                if b is None and g == 0:
                    pe.wait_ge(wT_ready, NH * f + 1)
                pe.wait_ge(fo_ev, NH * f + g + 1)
                transposes(bank, lambda t: OF[:, g, t * P:(t + 1) * P]).then_inc(fT_ps, 1)

            def body(b, first, last=False):
                f = b - 1
                for k in range(STEPS):
                    if last or k not in (SCORES_AT + 1, SCORES_AT + 2):
                        if not first or k >= 3:
                            projections(f, k, first)
                        if first and k == 0:
                            weightsT(f, 0, alone=True)
                            keys(b, 0)
                        if k >= LAG_W:
                            weights(f, k - LAG_W, first)
                        if k >= LAG_D and (last or k != SCORES_AT + 3):
                            down(f, k - LAG_D, first)
                        elif k < LAG_D and not first:
                            down(f - 1, STEPS + k - LAG_D, False)
                    if k == 5:
                        weightsT(f, 1, last=last)
                    if k == (6 if last else 18) and not first:
                        fT(f - 1, 1, None if last else b)
                    if k == (18 if last else 20):
                        fT(f, 0, None if last else b)
                    if last:
                        continue
                    if k == 1:
                        values(b, 0)
                        yT(b, 1)
                    if k == 4:
                        keys(b, 1)
                    if k == 6:
                        values(b, 1)
                    if k == SCORES_AT:
                        scores(b, 0)
                        scores(b, 1)
                        projections(f, k + 1, first)
                        scores(b, 2)
                        weights(f, k, first)
                        scores(b, 3)
                        down(f, k + 1 - LAG_D, first)
                        scores(b, 4)
                        scores(b, 5)
                        projections(f, k + 2, first)
                        scores(b, 6)
                        scores(b, 7)
                        weights(f, k + 1, first)
                        down(f, k + 2 - LAG_D, first)
                        scores(b, 8)
                        scores(b, 9)
                        scores(b, 10)
                        scores(b, 11)
                        down(f, k + 3 - LAG_D, first)
                        max_row(b)
                        max_all(b)
                        sum_all(b)
                    if k == 7:
                        attend(b, 0, 0, TPH)
                    if k == 8:
                        attend(b, 1, 0, 2)
                        oT(b, 0)
                        attend(b, 1, 2, NT)
                    if k == 9:
                        oT(b, 1)
                    if k == 14:
                        y2T(b, 0)
                    if k == 16:
                        y2T(b, 1)
                    if k == 21:
                        gate(b, alone=first)
                    if k == 22:
                        yT(b + 1, 0)
                    if k == 25:
                        keys(b + 1, 0)
                    if k == 27:
                        weightsT(b, 0)

            yT(0, 0, alone=True)
            yT(0, 1, alone=True)
            pe.wait_ge(prep_dve, 1)
            keys(0, 0)
            keys(0, 1)
            pe.wait_ge(identb_ready, 1)
            pe.wait_ge(values_loaded, 32)
            for u in range(NU):
                scores(0, u, alone=True)
                if u == 5:
                    values(0, 0, alone=True)
                if u == 7:
                    values(0, 1, alone=True)
            max_row(0)
            max_all(0)
            sum_all(0)
            attend(0, 0, 0, TPH)
            attend(0, 1, 0, 2)
            oT(0, 0)
            attend(0, 1, 2, NT)
            oT(0, 1)
            y2T(0, 0)
            pe.wait_ge(wgu_split, 2)
            projections(0, 0, True)
            y2T(0, 1)
            gate(0, alone=True)
            projections(0, 1, True)
            yT(1, 0)
            projections(0, 2, True)
            pe.wait_ge(consts, 2)
            body(1, True)
            with pe.Fori(2, NB) as b:
                body(b, False)
            body(NB, False, last=True)
            for k in range(STEPS - LAG_D, STEPS):
                down(NB - 1, k, False)
            fT(NB - 1, 1)

        @block.scalar
        def _(act):
            act.wait_ge(ident_ready, 1)
            nc.scalar.activation(identb[:, :], ident[:, :], ACT.Copy).then_inc(identb_ready, 1)
            act.wait_ge(small_loaded, 16 * 5)
            act.wait_ge(consts, 1)
            act.wait_ge(prep_ps, 1)
            nc.scalar.activation(bq_rep[:, :], ones[:, :], ACT.Copy, scale=bqk[:, 0:1])
            nc.scalar.activation(gwT_s[:, :], SC[0][:, 2 * P:2 * P + NE], ACT.Copy)
            nc.scalar.activation(WqkT[:, :, :], SC[0][:, 0:2 * P].rearrange("p (a n) -> p a n", a=2), ACT.Copy
                                 ).then_inc(prep_act, 1)

            def yT(b, h, alone=False):
                if h == 1 and not alone:
                    act.wait_ge(y2_moved, b)
                act.wait_ge(yT_ps, NH * b + h + 1)
                c = slice(h * HALF, (h + 1) * HALF)
                nc.scalar.activation(YF[:, c], SC[h][:, :], ACT.Copy)
                nc.scalar.activation(YT_h[:, c], SC[h][:, :], ACT.Copy).then_inc(yhi, 1)

            def keys(b, h):
                act.wait_ge(kk_ps, NH * b + h + 1)
                nc.scalar.activation(KK_h[:, h * HALF:(h + 1) * HALF], SC[h][:, :], ACT.Identity,
                                     bias=wqbk[:, :]).then_inc(khi, 1)

            def move_second_half(f, first):
                c = slice(HALF, T)
                if not first:
                    act.wait_ge(u_ps, f * STEPS)
                act.wait_ge(y2lo, NH * (f + 1))
                nc.scalar.activation(Y2_h[:, c], YT_h[:, c].bitcast(F32), ACT.Copy)
                nc.scalar.activation(Y2_l[:, c], YT_l[:, c].bitcast(F32), ACT.Copy).then_inc(y2_moved, 1)

            def exps(b, u):
                c0 = UNIT_COL[u]
                act.wait_ge(nb, NU * b + u + 1)
                nc.scalar.activation(E[:, UNIT_AT[u]:UNIT_AT[u] + HALF - c0], score_bank(b, u)[:, c0:HALF], ACT.Exp,
                                     bias=nbias[:, u:u + 1], accum_out=rsum[:, u:u + 1]
                                     ).then_inc(exps_done, 1)

            def factor(b):
                act.wait_ge(nmg_ready, b + 1)
                nc.scalar.activation(fac[:, :], val[:, :], ACT.Exp, bias=nmg[:, :]).then_inc(fexp, 1)

            def evacuate(b, h):
                act.wait_ge(pv_ps, NH * b + h + 1)
                nc.scalar.activation(OT[:, h * HALF:(h + 1) * HALF], SC[1 - h][:, :], ACT.Copy).then_inc(o_ev, 1)

            def y2T(b, h, alone=False):
                if h == 0 and not alone:
                    act.wait_ge(u_ps, (b - 1) * STEPS + NC)
                act.wait_ge(y2T_ps, NH * b + h + 1)
                dst = [Y2_h, YT_h][h]
                c = slice(h * HALF, (h + 1) * HALF)
                nc.scalar.activation(YF[:, c], SC[h][:, :], ACT.Copy).then_inc(y2whole, 1)
                nc.scalar.activation(dst[:, c], SC[h][:, :], ACT.Copy).then_inc(y2hi, 1)

            def gate(b):
                act.wait_ge(lg_ready, b + 1)
                nc.scalar.activation(eg[:, :, :], lg[:, :, :], ACT.Exp).then_inc(gexp, 1)

            def upper(f, k, first):
                r = rows(k % NC)
                act.wait_ge(h_ready, f * STEPS + k + 1)
                if k >= RING or not first:
                    act.wait_ge(d_ps, f * STEPS + k + 1 - RING)
                nc.scalar.activation(H_h[0:r, k % RING, :], H[0:r, k % RING, :], ACT.Copy).then_inc(hi_ready, 1)

            def weights(f, k, first):
                i = wb_count(k) - 1
                act.wait_ge(wb_ps, f * ROUTED_STEPS + i + 1)
                if i >= 2 or not first:
                    act.wait_ge(h_ready, f * STEPS + routed_step(i - 2) + 1)
                nc.scalar.activation(WS[:, i % 2, :], WB[:, :], ACT.Copy).then_inc(ws_ready, 1)

            def silu(f, k, first):
                r = rows(k % NC)
                act.wait_ge(g_ps, f * STEPS + k + 1)
                if k >= 2 and (k - 2) % NC < NR:
                    act.wait_ge(u_used, f * ROUTED_STEPS + wb_count(k - 2))
                elif k >= 2 or not first:
                    act.wait_ge(h_ready, f * STEPS + k - 1)
                nc.scalar.activation(S[0:r, k % 2, :], GB[k % 2][0:r, :], ACT.Silu).then_inc(s_ready, 1)

            def ffn_evacuate(f, g):
                act.wait_ge(d_ps, f * STEPS + (g + 1) * NC)
                nc.scalar.activation(OF[:, g, :], DB[:, :], ACT.Copy).then_inc(fo_ev, 1)

            def body(b, first, last=False):
                f = b - 1
                for k in range(STEPS):
                    if k == 4 and not first:
                        ffn_evacuate(f - 1, 1)
                    if k == 18:
                        ffn_evacuate(f, 0)
                    if not first or k >= 2:
                        silu(f, k, first)
                    if 0 < k % NC <= NR and (last or k not in (SCORES_AT + 1, SCORES_AT + 2)):
                        weights(f, k - LAG_W, first)
                    if k >= LAG_H:
                        if last or k not in (SCORES_AT + 1, SCORES_AT + 2):
                            upper(f, k - LAG_H, first)
                    elif not first:
                        upper(f - 1, STEPS + k - LAG_H, False)
                    if first and k == 0:
                        keys(b, 0)
                    if k == 0:
                        move_second_half(f, first)
                    if last:
                        continue
                    if k == 1:
                        yT(b, 1)
                    if k == 4:
                        keys(b, 1)
                    if k == SCORES_AT:
                        for u in range(NU):
                            exps(b, u)
                            if u == 1:
                                upper(f, k + 1 - LAG_H, first)
                            if u == 3:
                                weights(f, k, first)
                            if u == 5:
                                upper(f, k + 2 - LAG_H, first)
                            if u == 6:
                                weights(f, k + 1, first)
                        factor(b)
                    if k == 8:
                        evacuate(b, 0)
                        evacuate(b, 1)
                    if k == 14:
                        y2T(b, 0)
                    if k == 16:
                        y2T(b, 1)
                    if k == 21:
                        gate(b)
                    if k == 22:
                        yT(b + 1, 0)
                    if k == 25:
                        keys(b + 1, 0)

            yT(0, 0)
            yT(0, 1, alone=True)
            act.wait_ge(prep_dve, 1)
            keys(0, 0)
            keys(0, 1)
            for u in range(NU):
                exps(0, u)
            factor(0)
            act.wait_ge(wu_loaded, 32)
            nc.scalar.activation(Wu_h[:, :], Wu_s[:, :], ACT.Copy).then_inc(wu_upper, 1)
            evacuate(0, 0)
            act.wait_ge(wd_loaded, 48)
            nc.scalar.activation(Wd_h[:, 0:NC - 1, :], Wd_s[:, 0:NC - 1, :], ACT.Copy)
            nc.scalar.activation(Wd_h[0:LASTC, NC - 1, :], Wd_s[0:LASTC, NC - 1, :], ACT.Copy).then_inc(wd_upper, 1)
            evacuate(0, 1)
            y2T(0, 0, alone=True)
            y2T(0, 1)
            gate(0)
            silu(0, 0, True)
            yT(1, 0)
            silu(0, 1, True)
            body(1, True)
            with act.Fori(2, NB) as b:
                body(b, False)
            body(NB, False, last=True)
            for k in range(STEPS - LAG_H, STEPS):
                upper(NB - 1, k, False)
            ffn_evacuate(NB - 1, 1)

        @block.vector
        def _(dve):
            v = nc.vector
            LN_STEPS = 4
            DVE_STEPS = 3 * NH * LN_STEPS + 5
            n = [0, 0]

            def step(ins):
                n[1] += 1
                ins.then_inc(dve_step, 1)
                dve.wait_ge(dve_step, n[0] * DVE_STEPS + NH * LN_STEPS + n[1])

            def begin(b):
                n[0], n[1] = b, -NH * LN_STEPS if isinstance(b, int) and b == 0 else 0

            m = [0]

            def prep(ins):
                m[0] += 1
                ins.then_inc(prep_step, 1)
                dve.wait_ge(prep_step, m[0])

            def merge(st, mu, dif, vs, ve, step):
                v.tensor_tensor(mu, st[:, :, 1], st[:, :, 4], ALU.add)
                v.tensor_tensor(dif, st[:, :, 1], st[:, :, 4], ALU.subtract)
                step(v.tensor_tensor(vs, st[:, :, 2], st[:, :, 5], ALU.add))
                v.tensor_scalar(mu, mu, 0.5, None, ALU.mult)
                step(v.scalar_tensor_tensor(dif, dif, 0.25, dif, ALU.mult, ALU.mult))
                step(v.scalar_tensor_tensor(ve, vs, 1.0 / D, dif, ALU.mult, ALU.add))

            def tiles(h):
                return slice(h * TPH, (h + 1) * TPH)

            def x_variance(slot, h, st, mu, dif, vs, ve):
                hs = tiles(h)
                for t in range(h * TPH, (h + 1) * TPH):
                    last = v.bn_stats(st[:, t, :], X[:, slot, t, :])
                step(last)
                merge(st[:, hs, :], mu[:, hs], dif[:, hs], vs[:, hs], ve[:, hs], step)
                return v.tensor_scalar(ve[:, hs], ve[:, hs], EPS, None, ALU.add)

            def normalise(slot, h, mu, rs):
                for i in range(h * TPH, (h + 1) * TPH):
                    last = v.tensor_scalar(Y[:, i, :], X[:, slot, i, :], mu[:, i:i + 1], rs[:, i:i + 1],
                                           ALU.subtract, ALU.mult)
                return last

            def ln1_variance(b, slot, h, alone=False):
                if h == 0:
                    if not alone:
                        dve.wait_ge(y_ready, NH * b)
                    if alone:
                        dve.wait_ge(x_first_half, 16)
                    else:
                        dve.wait_ge(x_loaded, 16 * NB)
                    v.memset(scratch[:, :], 0.0)
                elif alone:
                    dve.wait_ge(x_loaded, 16)
                x_variance(slot, h, st_x, mu_x, dif_x, vs_x, ve_x).then_inc(var1, 1)

            def ln1(b, slot, h, alone=False):
                if not alone:
                    dve.wait_ge(y2T_ps, NH * b)
                dve.wait_ge(pow1, NH * b + h + 1)
                normalise(slot, h, mu_x, rs_x).then_inc(y_ready, 1)

            def yT(b, h):
                c = slice(h * HALF, (h + 1) * HALF)
                dve.wait_ge(yhi, NH * b + h + 1)
                v.tensor_tensor(YT_l[:, c], SC[h][:, :], YT_h[:, c].bitcast(F32), ALU.subtract).then_inc(ylo, 1)

            def keys(b, h):
                c = slice(h * HALF, (h + 1) * HALF)
                dve.wait_ge(khi, NH * b + h + 1)
                v.scalar_tensor_tensor(KK_l[:, c], SC[h][:, :], wqbk[:, :], KK_h[:, c].bitcast(F32),
                                       ALU.add, ALU.subtract).then_inc(klo, 1)

            def values(b, h, alone=False):
                bank = [WB, DB][h] if alone else SC[h]
                dve.wait_ge(v_ps, NH * b + h + 1)
                v.tensor_tensor(V[:, h * TPH:(h + 1) * TPH, :], bank[:, :].rearrange("p (t d) -> p t d", d=P),
                                bv_b[:, None, :].to_broadcast([P, TPH, P]), ALU.add).then_inc(v_ev, 1)

            def key_terms(b):
                dve.wait_ge(c_products, NH * (b + 1))
                step(v.tensor_reduce(cs[:, :], OT[:, :].rearrange("p (t d) -> p t d", d=P), AX.X, ALU.add))
                v.tensor_scalar(cs[:, :], cs[:, :], bqbk[:, :], SCALE, ALU.add, ALU.mult).then_inc(c_ev, 1)

            def shift(b, u):
                dve.wait_ge(sc_ps, NU * b + u + 1)
                v.tensor_reduce(nbias[:, u:u + 1], score_bank(b, u)[:, UNIT_COL[u]:HALF], AX.X, ALU.max, negate=True
                                ).then_inc(nb, 1)

            def maximum(b):
                dve.wait_ge(nb, NU * (b + 1))
                dve.wait_ge(c_ev, b + 1)
                v.tensor_tensor(val[:, 0:TPH], cs[:, 0:TPH], nbias[:, 0:TPH], ALU.subtract)
                step(v.tensor_tensor(val[:, TPH:NU], cs[:, :], nbias[:, TPH:NU], ALU.subtract))
                v.tensor_reduce(mx[:, :], val[:, :], AX.X, ALU.max).then_inc(mx_ready, 1)
                dve.wait_ge(maxT_ps, b + 1)
                v.tensor_reduce(m1[:, :], SC[0][0:1, 0:P], AX.X, ALU.max).then_inc(m1_ready, 1)
                dve.wait_ge(maxB_ps, b + 1)
                v.tensor_scalar(nmg[:, :], SC[0][:, P:P + 1], -1.0, None, ALU.mult).then_inc(nmg_ready, 1)

            def sums(b):
                dve.wait_ge(fexp, b + 1)
                dve.wait_ge(exps_done, NU * (b + 1))
                step(v.tensor_tensor(rf[:, :], rsum[:, :], fac[:, :], ALU.mult))
                v.tensor_reduce(zp[:, :], rf[:, :], AX.X, ALU.add).then_inc(zp_ready, 1)

            def scale_values(b, h):
                u0, k = (0, TPH) if h == 0 else (TPH, NT)
                v.tensor_tensor(VP[:, u0:u0 + k, :], V[:, 0:k, :],
                                fac[:, u0:u0 + k, None].to_broadcast([P, k, P]), ALU.mult).then_inc(vp_ready, 1)

            def epsilon(b):
                dve.wait_ge(z_ps, b + 1)
                step(v.tensor_copy(zs[:, :], SC[0][:, P:P + 1]))
                v.tensor_scalar(ez[:, :], zs[:, :], zs[:, :], EPS, ALU.mult, ALU.mult).then_inc(ez_ready, 1)

            def o_variance(b, h):
                hs = tiles(h)
                dve.wait_ge(oT_ps, NH * b + h + 1)
                for t in range(TPH):
                    last = v.bn_stats(st[:, h * TPH + t, :], SC[1 - h][:, t * P:(t + 1) * P])
                step(last)
                merge(st[:, hs, :], mu[:, hs], dif[:, hs], vs[:, hs], ve[:, hs], step)
                dve.wait_ge(ez_ready, b + 1)
                v.tensor_scalar(ve[:, hs], ve[:, hs], ez[:, :], None, ALU.add).then_inc(var2, 1)
                v.tensor_tensor(Y[:, hs, :], SC[1 - h][:, :].rearrange("p (t d) -> p t d", d=P),
                                mu[:, hs, None].to_broadcast([P, TPH, P]), ALU.subtract).then_inc(o_centred, 1)

            def x1(b, h):
                dve.wait_ge(pow2, NH * b + h + 1)
                dve.wait_ge(o_centred, NH * b + h + 1)
                for i in range(h * TPH, (h + 1) * TPH):
                    last = v.scalar_tensor_tensor(X[:, b, i, :], Y[:, i, :], rs[:, i:i + 1], X[:, b, i, :],
                                                  ALU.mult, ALU.add)
                last.then_inc(x1_ready, 1)
                dve.wait_ge(x1_ready, NH * b + h + 1)
                v.memset(scratch[:, :], 0.0)
                x_variance(b, h, st, mu, dif, vs, ve).then_inc(var3, 1)

            def ln2(b, h):
                dve.wait_ge(pow3, NH * b + h + 1)
                normalise(b, h, mu, rs).then_inc(y2_ready, 1)

            def y2T(b, h):
                c = slice(h * HALF, (h + 1) * HALF)
                dve.wait_ge(y2hi, NH * b + h + 1)
                hi, lo = [(Y2_h, Y2_l), (YT_h, YT_l)][h]
                v.tensor_tensor(lo[:, c], SC[h][:, :], hi[:, c].bitcast(F32), ALU.subtract).then_inc(y2lo, 1)

            full = [P, NT, NE]
            cube = [P, NT, NE, NE]

            def logits(b):
                dve.wait_ge(gate_ps, b + 1)
                lo_ = SC[0][:, 0:NT * NE].rearrange("p (t e) -> p t e", e=NE)
                step(v.tensor_reduce(gmax[:, :], lo_, AX.X, ALU.max))
                v.tensor_tensor(lg[:, :, :], lo_, gmax[:, :, None].to_broadcast(full), ALU.subtract
                                ).then_inc(lg_ready, 1)

            GATE_STEPS = 12

            def gate_state(b, h):
                count = [0]
                half = slice(h * TPH, (h + 1) * TPH)
                full = [P, TPH, NE]
                cube = [P, TPH, NE, NE]

                def gstep(ins):
                    count[0] += 1
                    ins.then_inc(gate_step, 1)
                    dve.wait_ge(gate_step, (NH * b + h) * GATE_STEPS + count[0])
                return count, half, full, cube, gstep

            def rank_experts(b, h):
                count, half, full, cube, gstep = gate_state(b, h)
                dve.wait_ge(gexp, b + 1)
                gstep(v.tensor_reduce(gsum[:, half], eg[:, half, :], AX.X, ALU.add))
                gstep(v.reciprocal(grec[:, half], gsum[:, half]))
                gstep(v.tensor_tensor(pg[:, half, :], eg[:, half, :], grec[:, half, None].to_broadcast(full), ALU.mult))
                other = pg[:, half, None, :].to_broadcast(cube)
                own = pg[:, half, :, None].to_broadcast(cube)
                v.tensor_tensor(cmp_gt[:, half, :, :], other, own, ALU.is_gt)
                gstep(v.tensor_tensor(cmp_eq[:, half, :, :], other, own, ALU.is_equal))
                v.tensor_tensor(cmp_eq[:, half, :, :], cmp_eq[:, half, :, :],
                                before[:, None, :, :].to_broadcast(cube), ALU.mult).then_inc(ties_ready, 1)

            def choose_experts(b, h):
                count, half, full, cube, gstep = gate_state(b, h)
                count[0] = 4
                dve.wait_ge(ties_ready, NH * b + h + 1)
                gstep(v.tensor_tensor(cmp_gt[:, half, :, :], cmp_gt[:, half, :, :], cmp_eq[:, half, :, :], ALU.add))
                gstep(v.tensor_reduce(rank[:, half, :], cmp_gt[:, half, :, :], AX.X, ALU.add))
                gstep(v.scalar_tensor_tensor(wsel[:, half, :], rank[:, half, :], 2.0, pg[:, half, :],
                                             ALU.is_lt, ALU.mult))
                gstep(v.tensor_reduce(gsum[:, half], wsel[:, half, :], AX.X, ALU.add))
                gstep(v.tensor_scalar(gsum[:, half], gsum[:, half], 1e-20, None, ALU.add))
                gstep(v.reciprocal(grec[:, half], gsum[:, half]))
                gstep(v.tensor_tensor(wn[:, half, :], wsel[:, half, :], grec[:, half, None].to_broadcast(full), ALU.mult))
                gstep(v.tensor_copy(whl[:, half, 0, :], wn[:, half, :]))
                assert count[0] == GATE_STEPS
                v.tensor_tensor(whl[:, half, 1, :], wn[:, half, :], whl[:, half, 0, :].bitcast(F32), ALU.subtract
                                ).then_inc(whl_ready, 1)

            def weightsT(b, h, alone=False):
                if h == 0 and not alone:
                    dve.wait_ge(wb_ps, (b - 1) * ROUTED_STEPS + NR)
                if h == 1 and not alone:
                    dve.wait_ge(wb_ps, b * ROUTED_STEPS)
                dve.wait_ge(wT_ps, NH * b + h + 1)
                v.tensor_copy(wT[:, h * HALF:(h + 1) * HALF], SC[1 - h][0:2 * NE, :]).then_inc(wT_ready, 1)

            def product(f, k, first):
                c, r = k % NC, rows(k % NC)
                dve.wait_ge(s_ready, f * STEPS + k + 1)
                dve.wait_ge(u_ps, f * STEPS + k + 1)
                if c < NR:
                    if c >= 2:
                        dve.wait_ge(h_ready, f * STEPS + k - 1)
                    v.tensor_tensor(TU[0:r, k % 2, :], S[0:r, k % 2, :], UB[k % 2][0:r, :], ALU.mult
                                    ).then_inc(u_used, 1)
                else:
                    if k >= RING or not first:
                        dve.wait_ge(lo_ready, f * STEPS + k + 1 - RING)
                    v.tensor_tensor(H[0:r, k % RING, :], S[0:r, k % 2, :], UB[k % 2][0:r, :], ALU.mult
                                    ).then_inc(h_ready, 1)

            def weigh(f, k, first):
                dve.wait_ge(u_used, f * ROUTED_STEPS + wb_count(k))
                dve.wait_ge(ws_ready, f * ROUTED_STEPS + wb_count(k))
                if k >= RING or not first:
                    dve.wait_ge(lo_ready, f * STEPS + k + 1 - RING)
                v.tensor_tensor(H[:, k % RING, :], TU[:, k % 2, :], WS[:, (wb_count(k) - 1) % 2, :],
                                ALU.mult).then_inc(h_ready, 1)

            F_STEPS = 4 * NH

            def ffn_ln(f, g):
                count = [0]

                def fstep(ins):
                    count[0] += 1
                    ins.then_inc(f_step, 1)
                    dve.wait_ge(f_step, f * F_STEPS + g * 4 + count[0])

                dve.wait_ge(fT_ps, NH * f + g + 1)
                for t in range(TPH):
                    last = v.bn_stats(fst[:, t, :], SC[1 - g][:, t * P:(t + 1) * P])
                fstep(last)
                merge(fst, fmu[:, :], fdif[:, :], fvs[:, :], fve[:, :], fstep)
                v.tensor_scalar(fve[:, :], fve[:, :], EPS, None, ALU.add).then_inc(var4, 1)
                v.tensor_tensor(FX[:, :, :], SC[1 - g][:, :].rearrange("p (t d) -> p t d", d=P),
                                fmu[:, :, None].to_broadcast([P, TPH, P]), ALU.subtract).then_inc(f_centred, 1)

            def ffn_out(f, g):
                dve.wait_ge(pow4, NH * f + g + 1)
                dve.wait_ge(f_centred, NH * f + g + 1)
                for t in range(TPH):
                    xo = X[:, f, g * TPH + t, :]
                    last = v.scalar_tensor_tensor(xo, FX[:, t, :], frs[:, t:t + 1], xo, ALU.mult, ALU.add)
                last.then_inc(out_ready, 1)

            def body(b, first, last=False):
                slot = (b + 1) % NB
                f = b - 1
                for k in range(STEPS):
                    if k % NC < NR and not (first and k < 2):
                        product(f, k, first)
                    if 0 < k % NC <= NR and (last or k != SCORES_AT + 1):
                        weigh(f, k - LAG_W, first)
                    if k % NC >= NR:
                        product(f, k, first)
                    if first and k == 0:
                        weightsT(f, 0, alone=True)
                        keys(b, 0)
                    if k == 0:
                        rank_experts(f, 1)
                    if k == 1:
                        choose_experts(f, 1)
                    if k == 5:
                        weightsT(f, 1, first)
                    if k == (7 if last else 18) and not first:
                        ffn_ln(f - 1, 1)
                    if k == (8 if last else 20) and not first:
                        ffn_out(f - 1, 1)
                    if k == (19 if last else 25):
                        ffn_ln(f, 0)
                    if k == (20 if last else 26):
                        ffn_out(f, 0)
                    if last:
                        continue
                    if k == 0:
                        begin(b)
                    if k == 2:
                        yT(b, 1)
                    if k == 3:
                        key_terms(b)
                        values(b, 0)
                    if k == 4:
                        keys(b, 1)
                    if k == SCORES_AT:
                        values(b, 1)
                        for u in range(NU):
                            shift(b, u)
                            if u == 4:
                                weigh(f, k, first)
                        maximum(b)
                        sums(b)
                        scale_values(b, 0)
                    if k == 6:
                        scale_values(b, 1)
                    if k == 7:
                        epsilon(b)
                    if k == 8:
                        o_variance(b, 0)
                        x1(b, 0)
                    if k == 9:
                        ln2(b, 0)
                    if k == 10:
                        o_variance(b, 1)
                    if k == 12:
                        x1(b, 1)
                    if k == 14:
                        ln1_variance(b + 1, slot, 0)
                        ln2(b, 1)
                    if k == 16:
                        ln1_variance(b + 1, slot, 1)
                    if k == 17:
                        y2T(b, 0)
                    if k == 18:
                        y2T(b, 1)
                    if k == 19:
                        ln1(b + 1, slot, 0)
                        ln1(b + 1, slot, 1)
                    if k == 21:
                        logits(b)
                        rank_experts(b, 0)
                    if k == 22:
                        choose_experts(b, 0)
                    if k == 23:
                        yT(b + 1, 0)
                    if k == 25:
                        keys(b + 1, 0)
                    if k == 27:
                        weightsT(b, 0)
                    if k == STEPS - 1:
                        assert n[1] == DVE_STEPS, n[1]

            begin(0)
            ln1_variance(0, 0, 0, alone=True)
            ln1_variance(0, 0, 1, alone=True)
            ln1(0, 0, 0, alone=True)
            ln1(0, 0, 1, alone=True)
            dve.wait_ge(prep_ps, 2)
            prep(v.tensor_scalar(A_h[:, :], GB[0][:, 0:P], SCALE, None, ALU.mult))
            v.scalar_tensor_tensor(A_l[:, :], GB[0][:, 0:P], SCALE, A_h[:, :].bitcast(F32), ALU.mult, ALU.subtract)
            v.tensor_scalar(wqbk[:, :], GB[0][:, P:P + 1], SCALE, None, ALU.mult)
            v.tensor_copy(bqbk[:, :], GB[0][:, P + 1:P + 2])
            v.tensor_copy(wkbq_rep[:, :], GB[0][:, 2 * P:3 * P]).then_inc(prep_dve, 1)
            yT(0, 0)
            yT(0, 1)
            key_terms(0)
            keys(0, 0)
            keys(0, 1)
            dve.wait_ge(values_loaded, 32)
            for u in range(NU):
                shift(0, u)
                if u == 5:
                    values(0, 0, alone=True)
                if u == 7:
                    values(0, 1, alone=True)
            maximum(0)
            sums(0)
            scale_values(0, 0)
            scale_values(0, 1)
            epsilon(0)
            ln1_variance(1, 1, 0)
            ln1_variance(1, 1, 1)
            o_variance(0, 0)
            x1(0, 0)
            o_variance(0, 1)
            ln2(0, 0)
            x1(0, 1)
            y2T(0, 0)
            ln2(0, 1)
            y2T(0, 1)
            ln1(1, 1, 0)
            ln1(1, 1, 1)
            logits(0)
            rank_experts(0, 0)
            product(0, 0, True)
            choose_experts(0, 0)
            yT(1, 0)
            product(0, 1, True)
            body(1, True)
            with dve.Fori(2, NB) as b:
                body(b, False)
            body(NB, False, last=True)
            ffn_ln(NB - 1, 1)
            ffn_out(NB - 1, 1)


_INS = ["L0_attn_x", "L0_attn_Wq", "L0_attn_bq", "L0_attn_Wk", "L0_attn_bk", "L0_attn_Wv", "L0_attn_bv",
        "L0_ffn_gate_w", "L0_ffn_wg", "L0_ffn_wu", "L0_ffn_wd", "L0_ffn_swg", "L0_ffn_swu", "L0_ffn_swd"]


def kernel(**inputs):
    import concourse.bacc as _bacc
    from concourse.bass_utils import run_bass_kernel_spmd as _run

    nc = _bacc.Bacc("TRN2", target_bir_lowering=False, num_devices=1)
    arrays, args = {}, []
    for name in _INS:
        a = np.ascontiguousarray(inputs[name])
        arrays[f"in_{name}"] = a
        args.append(nc.dram_tensor(f"in_{name}", a.shape, mybir.dt.from_np(a.dtype), kind="ExternalInput").ap())
    args.append(nc.dram_tensor("out_0", (NB, T, D), F32, kind="ExternalOutput").ap())
    sandwich(nc, *args)
    r = _run(nc, [arrays], core_ids=[0])
    return r.results[0]["out_0"]
```
